# Optimizing a Trainium2 kernel written in Bass

```python
import numpy as np
import jax
import jax.numpy as jnp

def _softmax(x, axis=-1):
    return jax.nn.softmax(x, axis=axis)

def _gelu(x):
    return jax.nn.gelu(x, approximate=True)

def _silu(x):
    return jax.nn.silu(x)

def _sigmoid(x):
    return jax.nn.sigmoid(x)

def _layernorm(x, axis=-1, eps=1e-05):
    m = jnp.mean(x, axis=axis, keepdims=True)
    v = jnp.var(x, axis=axis, keepdims=True)
    return (x - m) / jnp.sqrt(v + eps)

def _scatter_add(tgt, idx, src, axis=0):
    return tgt.at[idx].add(src)

def _segment_sum(src, seg, n):
    return jax.ops.segment_sum(src, seg, n)
kernel_name = 'mk_lm_tower_d1_tok_ids1024_r4_bd1f98'

def setup_inputs(seed: int=0):
    np.random.seed(seed)
    _w = jnp.asarray

    def _rec_inputs():
        import jax
        import jax.numpy as jnp
        _rk = jax.random.key(seed)
        x = jax.random.randint(jax.random.fold_in(_rk, 1), (32, 128), 0, 267694, jnp.int32)
        return x
    x = _rec_inputs()

    def _L0_tok_setup():
        import jax, jax.numpy as jnp
        import numpy as np
        N_TOKEN = 267735
        D_EMBED = 256
        D_PROJ = 256
        DIV_VAL = 4
        CUTOFF_ENDS = [0, 5000, 10000, 50000, N_TOKEN]
        N_BUCKETS = 4
        key = jax.random.key(seed)
        keys = jax.random.split(key, 1 + 2 * N_BUCKETS)
        inp = {}
        inp['input_ids'] = jax.random.randint(keys[0], (8, 512), 0, N_TOKEN, dtype=jnp.int64 if jax.config.jax_enable_x64 else jnp.int32)
        for i in range(N_BUCKETS):
            l, r = (CUTOFF_ENDS[i], CUTOFF_ENDS[i + 1])
            d_i = D_EMBED // DIV_VAL ** i
            inp[f'emb{i}'] = jax.random.normal(keys[1 + i], (r - l, d_i), dtype=jnp.float32)
            s = 1.0 / np.sqrt(d_i)
            inp[f'proj{i}'] = jax.random.uniform(keys[1 + N_BUCKETS + i], (D_PROJ, d_i), dtype=jnp.float32, minval=-s, maxval=s)
        return inp
    _L0_tok_all = _L0_tok_setup()
    _L0_tok_in = {k: v for k, v in _L0_tok_all.items() if k in ('emb0', 'emb1', 'emb2', 'emb3', 'proj0', 'proj1', 'proj2', 'proj3')}
    del _L0_tok_all

    def _L0_attn_setup():
        import jax, jax.numpy as jnp
        import numpy as np
        B, S, E, H = (2, 512, 256, 16)
        D = E // H
        NEG_INF = -1e+30

        def alibi_slopes(n_head):
            return jnp.asarray([2.0 ** (-8.0 * (i + 1) / n_head) for i in range(n_head)], dtype=jnp.float32)
        key = jax.random.key(seed)
        ks = jax.random.split(key, 5)
        scale = 0.02
        return {'x': jax.random.normal(ks[0], (B, S, E), dtype=jnp.float32), 'W_kqv': jax.random.normal(ks[1], (E, 3 * E), dtype=jnp.float32) * scale, 'b_kqv': jnp.zeros((3 * E,), dtype=jnp.float32), 'W_proj': jax.random.normal(ks[2], (E, E), dtype=jnp.float32) * scale, 'b_proj': jnp.zeros((E,), dtype=jnp.float32), 'slopes': alibi_slopes(H)}
    _L0_attn_all = _L0_attn_setup()
    _L0_attn_in = {k: v for k, v in _L0_attn_all.items() if k in ('W_kqv', 'b_kqv', 'W_proj', 'b_proj', 'slopes')}
    del _L0_attn_all

    def _L0_ffn_setup():
        import jax, jax.numpy as jnp
        import numpy as np
        TOP_K = 8
        NUM_EXPERTS = 32
        CAPACITY = 256
        key = jax.random.key(seed)
        k1, k2, k3, k4 = jax.random.split(key, 4)
        B, S, H, E, F = (2, 256, 256, NUM_EXPERTS, 192)
        return {'hidden_states': jax.random.normal(k1, (B, S, H), dtype=jnp.float32), 'gate_weight': jax.random.normal(k2, (E, H), dtype=jnp.float32) * 0.02, 'gate_up_proj': jax.random.normal(k3, (E, 2 * F, H), dtype=jnp.float32) * 0.02, 'down_proj': jax.random.normal(k4, (E, H, F), dtype=jnp.float32) * 0.02}
    _L0_ffn_all = _L0_ffn_setup()
    _L0_ffn_in = {k: v for k, v in _L0_ffn_all.items() if k in ('gate_weight', 'gate_up_proj', 'down_proj')}
    del _L0_ffn_all
    return {'x': x, 'L0_tok_emb0': _L0_tok_in['emb0'], 'L0_tok_emb1': _L0_tok_in['emb1'], 'L0_tok_emb2': _L0_tok_in['emb2'], 'L0_tok_emb3': _L0_tok_in['emb3'], 'L0_tok_proj0': _L0_tok_in['proj0'], 'L0_tok_proj1': _L0_tok_in['proj1'], 'L0_tok_proj2': _L0_tok_in['proj2'], 'L0_tok_proj3': _L0_tok_in['proj3'], 'L0_attn_W_kqv': _L0_attn_in['W_kqv'], 'L0_attn_b_kqv': _L0_attn_in['b_kqv'], 'L0_attn_W_proj': _L0_attn_in['W_proj'], 'L0_attn_b_proj': _L0_attn_in['b_proj'], 'L0_attn_slopes': _L0_attn_in['slopes'], 'L0_ffn_gate_weight': _L0_ffn_in['gate_weight'], 'L0_ffn_gate_up_proj': _L0_ffn_in['gate_up_proj'], 'L0_ffn_down_proj': _L0_ffn_in['down_proj']}

def reference(x, L0_tok_emb0, L0_tok_emb1, L0_tok_emb2, L0_tok_emb3, L0_tok_proj0, L0_tok_proj1, L0_tok_proj2, L0_tok_proj3, L0_attn_W_kqv, L0_attn_b_kqv, L0_attn_W_proj, L0_attn_b_proj, L0_attn_slopes, L0_ffn_gate_weight, L0_ffn_gate_up_proj, L0_ffn_down_proj):
    import jax
    import jax.numpy as jnp

    def _L0_tok_ref(input_ids, emb0, emb1, emb2, emb3, proj0, proj1, proj2, proj3):
        import jax, jax.numpy as jnp
        import numpy as np
        N_TOKEN = 267735
        D_EMBED = 256
        D_PROJ = 256
        DIV_VAL = 4
        CUTOFF_ENDS = [0, 5000, 10000, 50000, N_TOKEN]
        N_BUCKETS = 4
        embs = [emb0, emb1, emb2, emb3]
        projs = [proj0, proj1, proj2, proj3]
        flat = input_ids.reshape(-1)
        out = jnp.zeros((flat.shape[0], D_PROJ), dtype=emb0.dtype)
        for i in range(N_BUCKETS):
            l, r = (CUTOFF_ENDS[i], CUTOFF_ENDS[i + 1])
            mask = (flat >= l) & (flat < r)
            idx = jnp.clip(flat - l, 0, r - l - 1)
            e = jnp.take(embs[i], idx, axis=0)
            p = jnp.einsum('nd,pd->np', e, projs[i])
            out = out + jnp.where(mask[:, None], p, jnp.zeros((), dtype=p.dtype))
        return out.reshape(*input_ids.shape, D_PROJ)

    def _L0_attn_ref(x, W_kqv, b_kqv, W_proj, b_proj, slopes):
        import jax, jax.numpy as jnp
        import numpy as np
        B, S, E, H = (2, 512, 256, 16)
        D = E // H
        NEG_INF = -1e+30

        def alibi_slopes(n_head):
            return jnp.asarray([2.0 ** (-8.0 * (i + 1) / n_head) for i in range(n_head)], dtype=jnp.float32)
        b, s, e = x.shape
        kqv = x @ W_kqv + b_kqv
        k, q, v = jnp.split(kqv, 3, axis=-1)
        k = k.reshape(b, s, H, D)
        q = q.reshape(b, s, H, D)
        v = v.reshape(b, s, H, D)
        attn = jnp.einsum('bqhd,bkhd->bhqk', q, k) * (1.0 / jnp.sqrt(jnp.float32(D)))
        i = jnp.arange(s)[:, None]
        j = jnp.arange(s)[None, :]
        rel = (j - i).astype(jnp.float32)
        bias = slopes[:, None, None] * jnp.tril(rel)
        bias = jnp.where(j > i, NEG_INF, bias)
        attn = jax.nn.softmax(attn + bias[None], axis=-1)
        y = jnp.einsum('bhqk,bkhd->bqhd', attn, v).reshape(b, s, e)
        return y @ W_proj + b_proj

    def _L0_ffn_ref(hidden_states, gate_weight, gate_up_proj, down_proj):
        import jax, jax.numpy as jnp
        import numpy as np
        TOP_K = 8
        NUM_EXPERTS = 32
        CAPACITY = 256
        B, S, H = hidden_states.shape
        E = gate_weight.shape[0]
        N = B * S
        x = hidden_states.reshape(N, H)
        logits = x @ gate_weight.T
        probs = jax.nn.softmax(logits.astype(jnp.float32), axis=-1)
        topw, topi = jax.lax.top_k(probs, TOP_K)
        topw = topw / topw.sum(-1, keepdims=True)
        topw = topw.astype(x.dtype)
        flat_e = topi.reshape(-1)
        flat_w = topw.reshape(-1)
        flat_x = jnp.repeat(x, TOP_K, axis=0)
        oh = jax.nn.one_hot(flat_e, E, dtype=jnp.int32)
        pos = (jnp.cumsum(oh, axis=0) * oh).sum(-1) - 1
        buf = jnp.zeros((E, CAPACITY, H), x.dtype).at[flat_e, pos].set(flat_x, mode='drop')
        gu = jnp.einsum('ech,efh->ecf', buf, gate_up_proj)
        gate, up = jnp.split(gu, 2, axis=-1)
        h = jax.nn.silu(gate) * up
        eo = jnp.einsum('ecf,ehf->ech', h, down_proj)
        tok_out = eo.at[flat_e, pos].get(mode='fill', fill_value=0)
        out = (tok_out * flat_w[:, None]).reshape(N, TOP_K, H).sum(1)
        return out.reshape(B, S, H)
    h = _L0_tok_ref(x, L0_tok_emb0, L0_tok_emb1, L0_tok_emb2, L0_tok_emb3, L0_tok_proj0, L0_tok_proj1, L0_tok_proj2, L0_tok_proj3)
    h = h + _L0_attn_ref(_layernorm(h, axis=-1), L0_attn_W_kqv, L0_attn_b_kqv, L0_attn_W_proj, L0_attn_b_proj, L0_attn_slopes)
    h = h + _L0_ffn_ref(_layernorm(h, axis=-1), L0_ffn_gate_weight, L0_ffn_gate_up_proj, L0_ffn_down_proj)
    return h

_drawn_inputs = setup_inputs


def setup_inputs(seed=0):
    import zlib

    import numpy as np

    out = dict(_drawn_inputs(seed))
    spreads = {'L0_attn_b_kqv': (0.0, 0.1), 'L0_attn_b_proj': (0.0, 0.1)}
    factors = {'L0_ffn_gate_weight': 8.0, 'L0_ffn_gate_up_proj': 8.0, 'L0_ffn_down_proj': 8.0}
    for name, (base, spread) in spreads.items():
        noise = np.random.default_rng([zlib.crc32(name.encode()), seed]).standard_normal(out[name].shape)
        drawn = base * np.exp(spread * noise) if base else spread * noise
        out[name] = jnp.asarray(drawn.astype(out[name].dtype))
    for name, factor in factors.items():
        out[name] = (out[name] * factor).astype(out[name].dtype)
    return out
```

```python
import concourse.bass as bass
from concourse import mybir
from contextlib import ExitStack


def bass_lm_tower_kernel(
    nc: bass.Bass,
    tokens: bass.AP,
    emb0: bass.AP,
    emb1: bass.AP,
    emb2: bass.AP,
    emb3: bass.AP,
    proj0: bass.AP,
    proj1: bass.AP,
    proj2: bass.AP,
    proj3: bass.AP,
    w_kqv: bass.AP,
    b_kqv: bass.AP,
    w_proj: bass.AP,
    b_proj: bass.AP,
    slopes: bass.AP,
    gate_weight: bass.AP,
    gate_up_proj: bass.AP,
    down_proj: bass.AP,
    out: bass.AP,
):
    fp32, bf16, i32 = mybir.dt.float32, mybir.dt.bfloat16, mybir.dt.int32
    ALU = mybir.AluOpType
    ACT = mybir.ActivationFunctionType
    AX = mybir.AxisListType

    P = 128
    NB, S = tokens.shape
    DM = emb0.shape[1]
    KC = DM // P
    NTOK = NB * S
    EMBS = [emb0, emb1, emb2, emb3]
    PROJS = [proj0, proj1, proj2, proj3]
    WIDTHS = [e.shape[1] for e in EMBS]
    STARTS = [sum(WIDTHS[:n]) for n in range(4)]
    FIRST_ID = [sum(e.shape[0] for e in EMBS[:n]) for n in range(4)]
    EW = sum(WIDTHS)
    ER = EW - KC * P
    H = slopes.shape[0]
    D = DM // H
    NC = 4
    HC = H // NC
    PAIRS = P // (2 * D)
    NE, F2, _ = gate_up_proj.shape
    F = F2 // 2
    F1 = F - P
    CAP = 256
    CC = CAP // P
    XW = DM + NE
    NEG = 1e30
    BIG = float(1 << 24)
    EPS = 1e-5
    QSCALE = -float(D) ** -0.5

    def head_of(c, j):
        return (j // 2) * 2 * PAIRS + 2 * c + j % 2

    xrow = nc.dram_tensor("xrow", (NTOK + CAP, XW), fp32).ap()
    counts_dram = nc.dram_tensor("counts_dram", (NB, NE, S), bf16).ap()

    ctx = ExitStack()
    with ctx:
        def sb(name, shape, dt=fp32):
            return ctx.enter_context(nc.sbuf_tensor(name, shape, dt))

        def pb(name, shape, dt=fp32):
            return ctx.enter_context(nc.psum_tensor(name, shape, dt))

        def sem(name):
            return ctx.enter_context(nc.semaphore(name))

        ident = sb("ident", [P, P])
        upper_f = sb("upper_f", [P, P])
        upper = sb("upper", [P, P], bf16)
        ones = sb("ones", [P, P], bf16)
        rel_i = sb("rel_i", [P, S], i32)
        rel = sb("rel", [P, S])
        later = sb("later", [P, S])
        bias_neg = sb("bias_neg", [P, NC, HC, S])
        slopes_b = sb("slopes_b", [P, H])
        slopes_n = sb("slopes_n", [P, H])
        minus_half = sb("minus_half", [P, 1])
        part_i = sb("part_i", [P, 1], i32)
        part_b = sb("part_b", [P, 1], i32)
        even = sb("even", [P, 1])
        odd = sb("odd", [P, 1])
        ids_rows = sb("ids_rows", [NB, S], i32)
        ids_f = sb("ids_f", [NB, S])
        ids_t = sb("ids_t", [P, NB])
        low = sb("low", [P, 4, NB])
        shifted = sb("shifted", [P, 4, NB])
        ids_all = sb("ids_all", [P, NB, 4], i32)
        proj_rows = sb("proj_rows", [P, KC, EW])
        projT = sb("projT", [P, KC, DM])
        projT_r = sb("projT_r", [ER, DM])
        gate_rows = sb("gate_rows", [NE, DM])
        gateT = sb("gateT", [P, KC, NE])
        bias_rows = sb("bias_rows", [3 * KC, P])
        bias_t = sb("bias_t", [P, 3 * KC])
        qbias = sb("qbias", [P, KC])
        kbias_even = sb("kbias_even", [P, KC])
        kbias_odd = sb("kbias_odd", [P, KC])
        vbias = sb("vbias", [P, DM])
        pbias = sb("pbias", [P, DM])
        wkqv = sb("wkqv", [P, KC, 3 * DM])
        wq = sb("wq", [P, KC, DM])
        wproj = sb("wproj", [P, KC, DM])
        zeros = sb("zeros", [P, CC, XW])

        idx = sb("idx", [P, 2, 4], i32)
        emb = sb("emb", [P, 2, EW])
        embT = sb("embT", [P, 2, (KC + 1) * P])
        h_all = sb("h_all", [P, NB, DM])
        hb = sb("hb", [P, 2, DM])
        st1 = sb("st1", [P, 2, 6])
        mv1 = sb("mv1", [P, 2, 2])
        ve1 = sb("ve1", [P, 2, 1])
        rs1 = sb("rs1", [P, 2, 1])
        ln1 = sb("ln1", [P, 2, DM])
        ln1T = sb("ln1T", [P, 2, DM])
        qT = sb("qT", [P, 2, KC, S])
        kT = sb("kT", [P, 2, KC, 2, S])
        vv = sb("vv", [P, 2, H, D + 1])
        sc = sb("sc", [P, 2, NC, HC, S])
        mn = sb("mn", [P, 2, NC, HC])
        pT = sb("pT", [P, 2, HC, S])
        rden = sb("rden", [P, 2, H])
        y = sb("y", [P, 2, DM])
        yT = sb("yT", [P, 2, DM])
        h1 = sb("h1", [P, 2, DM])
        st2 = sb("st2", [P, 2, 6])
        mv2 = sb("mv2", [P, 2, 2])
        ve2 = sb("ve2", [P, 2, 1])
        rs2 = sb("rs2", [P, 2, 1])
        xr = sb("xr", [P, 2, XW])
        ln2T = sb("ln2T", [P, 2, DM])
        logits = sb("logits", [P, 2, NE])
        top8 = sb("top8", [P, 2, 8])
        nmax = sb("nmax", [P, 2, 1])
        rest = sb("rest", [P, 2, NE])
        ex = sb("ex", [P, 2, NE])
        mask = sb("mask", [P, 2, NE], bf16)
        seen = sb("seen", [P, 2, NE], bf16)
        exm = sb("exm", [P, 2, NE])
        esum = sb("esum", [P, 2, 1])
        rsum = sb("rsum", [P, 2, 1])
        cnt = sb("cnt", [NE, 2, S], bf16)

        cum = sb("cum", [NB, NE, S], bf16)
        cum_p = sb("cum_p", [NB, NE, S], bf16)
        slot_i = sb("slot_i", [NB, CAP], i32)
        slot_row = sb("slot_row", [NB, CAP])
        seq_i = sb("seq_i", [NB, 1], i32)
        seq_col = sb("seq_col", [NB, 2], bf16)
        slotp_i = sb("slotp_i", [P, CC], i32)
        slotp = sb("slotp", [P, CC])
        spare = sb("spare", [P, CC])
        before = sb("before", [NB, 2, CAP])
        onehot = sb("onehot", [NB, 2, CAP], bf16)
        le = sb("le", [P, 2, CC, S])
        nle = sb("nle", [P, 2, CC])
        t_a = sb("t_a", [P, 2, CC])
        t_b = sb("t_b", [P, 2, CC])
        t_c = sb("t_c", [P, 2, CC])
        rows_all = sb("rows_all", [P, NE, CC], i32)
        gidx = sb("gidx", [P, 2, CC], i32)
        sidx = sb("sidx", [P, 2, CC], i32)
        xg = sb("xg", [P, 2, CC, XW])
        xgT = sb("xgT", [P, 2, KC, CAP])
        wcol = sb("wcol", [P, 2, CC])
        gu = sb("gu", [P, 2, F2 // P, DM])
        dn = sb("dn", [P, 2, KC, F])
        guT = sb("guT", [P, 2, KC, F2])
        dnT = sb("dnT", [P, 2, 2, DM])
        silu_a = sb("silu_a", [P, CAP])
        silu_b = sb("silu_b", [F1, CAP])
        hT_a = sb("hT_a", [P, CAP])
        hT_b = sb("hT_b", [F1, CAP])
        eo = sb("eo", [P, 2, CC, DM])

        bank = [pb(f"bank{n}", [P, 512]) for n in range(8)]
        score_ps = bank[0:2]
        q_ps = bank[0][:, 0:KC * S].rearrange("p (c s) -> p c s", c=KC)
        k_ps = bank[0][:, KC * S:2 * KC * S].rearrange("p (c s) -> p c s", c=KC)
        v_ps = bank[1][:, 0:DM]
        probT_ps = bank[2:4]
        embT_ps, h_ps, ln2T_ps = bank[4], bank[4][:, 0:DM], bank[4][:, 0:DM]
        yT_ps, ln1T_ps = bank[5][:, 0:DM], bank[5][:, 0:DM]
        proj_ps = bank[6][:, 0:DM]
        logit_ps = bank[6][:, 256:256 + NE]
        cnt_ps = bank[6][0:NE, 384:384 + S]
        y_ps = bank[7][:, 0:H * (D + 1)].rearrange("p (h d) -> p h d", h=H)
        gate_ps, mixed_ps, up_ps = bank[0][:, 0:CAP], bank[1][:, 0:CAP], bank[2][:, 0:CAP]
        cumrow_ps = bank[2][:, CAP:CAP + CC * S].rearrange("p (c s) -> p c s", c=CC)
        base_ps = bank[1][:, CAP:CAP + 2 * CC].rearrange("p (c k) -> p c k", c=CC)
        eo_ps = bank[3]
        guT_ps = bank[4:6]
        dnT_ps = bank[6]
        xgT_ps = bank[7]

        weights_in = sem("weights_in")
        ids_in = sem("ids_in")
        small_in = sem("small_in")
        pool_const = sem("pool_const")
        pool_step = sem("pool_step")
        ids_float = sem("ids_float")
        setup_T = sem("setup_T")
        dve_step = sem("dve_step")
        ids_ready = sem("ids_ready")
        proj_ready = sem("proj_ready")
        setup_ready = sem("setup_ready")
        zeros_ready = sem("zeros_ready")
        spare_out = sem("spare_out")
        emb_clear = sem("emb_clear")
        idx_copied = sem("idx_copied")
        gathered = [sem(f"gathered{n}") for n in range(2)]
        embT_done = sem("embT_done")
        embT_copied = sem("embT_copied")
        h_done = sem("h_done")
        h_copied = sem("h_copied")
        st1_done = sem("st1_done")
        mv1_done = sem("mv1_done")
        var1_ready = sem("var1_ready")
        rs1_ready = sem("rs1_ready")
        hb_ready = sem("hb_ready")
        ln1_ready = sem("ln1_ready")
        ln1T_done = sem("ln1T_done")
        ln1T_copied = sem("ln1T_copied")
        qk_done = sem("qk_done")
        qk_ready = sem("qk_ready")
        v_done = sem("v_done")
        v_ready = sem("v_ready")
        score_done = sem("score_done")
        score_read = sem("score_read")
        min_ready = sem("min_ready")
        prob_ready = sem("prob_ready")
        probT_done = sem("probT_done")
        probT_copied = sem("probT_copied")
        pv_done = sem("pv_done")
        rden_ready = sem("rden_ready")
        y_ready = sem("y_ready")
        yT_done = sem("yT_done")
        yT_copied = sem("yT_copied")
        proj_done = sem("proj_done")
        h1_ready = sem("h1_ready")
        st2_done = sem("st2_done")
        mv2_done = sem("mv2_done")
        var2_ready = sem("var2_ready")
        rs2_ready = sem("rs2_ready")
        ln2_ready = sem("ln2_ready")
        ln2T_done = sem("ln2T_done")
        ln2T_copied = sem("ln2T_copied")
        logit_done = sem("logit_done")
        logit_copied = sem("logit_copied")
        top8_ready = sem("top8_ready")
        nmax_ready = sem("nmax_ready")
        rest_ready = sem("rest_ready")
        mask_ready = sem("mask_ready")
        seen_ready = sem("seen_ready")
        ex_ready = sem("ex_ready")
        exm_ready = sem("exm_ready")
        rsum_ready = sem("rsum_ready")
        row_ready = sem("row_ready")
        cnt_done = sem("cnt_done")
        cnt_copied = sem("cnt_copied")
        h1_out = [sem(f"h1_out{n}") for n in range(2)]
        row_out = [sem(f"row_out{n}") for n in range(2)]
        cnt_out = [sem(f"cnt_out{n}") for n in range(2)]
        cum_in = sem("cum_in")
        cum_clear = sem("cum_clear")
        slots_ready = sem("slots_ready")
        before_ready = sem("before_ready")
        onehot_ready = sem("onehot_ready")
        rows_done = sem("rows_done")
        count_ready = sem("count_ready")
        row_a = sem("row_a")
        row_b = sem("row_b")
        row_c = sem("row_c")
        rows_ready = sem("rows_ready")
        gidx_copied = sem("gidx_copied")
        sidx_copied = sem("sidx_copied")
        xg_in = [sem(f"xg_in{n}") for n in range(2)]
        gu_in = [sem(f"gu_in{n}") for n in range(2)]
        dn_in = [sem(f"dn_in{n}") for n in range(2)]
        guT_done = sem("guT_done")
        dnT_done = sem("dnT_done")
        wT_copied_act = sem("wT_copied_act")
        wT_copied_dve = sem("wT_copied_dve")
        xgT_done = sem("xgT_done")
        xgT_copied = sem("xgT_copied")
        wcol_ready = sem("wcol_ready")
        gate_done = sem("gate_done")
        silu_ready = sem("silu_ready")
        hT_ready = sem("hT_ready")
        eo_done = sem("eo_done")
        eo_ready = sem("eo_ready")
        added = [sem(f"added{n}") for n in range(2)]

        block = ctx.enter_context(nc.Block())

        AHEAD, BEHIND = 3, 3
        FULL_LO, FULL_HI = BEHIND + 3, NB - AHEAD - 1

        def steps(eng, step):
            for i in range(-AHEAD, FULL_LO):
                step(i, i % 2, lambda lag, i=i: 0 <= i + lag < NB)
            with eng.Fori(FULL_LO // 2, FULL_HI // 2) as t:
                for par in range(2):
                    step(2 * t + par, par, lambda lag: True)
            for i in range(FULL_HI, NB + BEHIND):
                step(i, i % 2, lambda lag, i=i: 0 <= i + lag < NB)

        def known(v):
            return isinstance(v, int)

        def wait(eng, s, v):
            if not known(v) or v > 0:
                eng.wait_ge(s, v)


        @block.sync
        def _(sp):
            sp.dma_start(ids_rows[:], tokens).then_inc(ids_in, 16)
            for n in range(4):
                sp.dma_start(proj_rows[:, :, STARTS[n]:STARTS[n] + WIDTHS[n]],
                             PROJS[n].rearrange("(c p) d -> p c d", p=P)).then_inc(small_in, 16)
            sp.dma_start(gate_rows[:], gate_weight).then_inc(small_in, 16)
            sp.dma_start(bias_rows[:], b_kqv.rearrange("(c p) -> c p", p=P)).then_inc(small_in, 16)
            sp.dma_start(slopes_b[:], slopes.partition_broadcast(P)).then_inc(small_in, 16)
            sp.dma_start(wkqv[:], w_kqv.rearrange("(c p) n -> p c n", p=P)).then_inc(weights_in, 16)
            sp.dma_start(wproj[:], w_proj.rearrange("(c p) n -> p c n", p=P)).then_inc(weights_in, 16)
            sp.dma_start(vbias[:], b_kqv[2 * DM:3 * DM].partition_broadcast(P)).then_inc(weights_in, 16)
            sp.dma_start(pbias[:], b_proj.partition_broadcast(P)).then_inc(weights_in, 16)
            sp.wait_ge(zeros_ready, 1)
            sp.dma_start(xrow[NTOK:NTOK + CAP, :].rearrange("(c p) w -> p c w", p=P), zeros[:]).then_inc(spare_out, 16)
            sp.dma_start(out[NTOK:NTOK + CAP, :].rearrange("(c p) w -> p c w", p=P),
                         zeros[:, :, 0:DM]).then_inc(spare_out, 16)

            def load(e, p, t):
                if not (known(e) and e < 2):
                    wait(sp, guT_done, e - 1)
                    wait(sp, dnT_done, e - 1)
                rows = gate_up_proj[bass.ds(e, 1), :, :].rearrange("e (a f) h -> f (e a) h", a=2)
                sp.dma_start(gu[:, p, 0:3:2, :], rows[0:P, :, :]).then_inc(gu_in[p], 16)
                for a in range(2):
                    sp.dma_start(gu[a * F1:(a + 1) * F1, p, 1, :], rows[P:F, a, :]).then_inc(gu_in[p], 16)
                sp.dma_start(dn[:, p, :, :], down_proj[bass.ds(e, 1), :, :].rearrange("e (c p) f -> p (e c) f", p=P)
                             ).then_inc(dn_in[p], 16)

            load(0, 0, 0)
            load(1, 1, 0)

            def step(i, par, has):
                if has(-3):
                    b, p = i - 3, 1 - par
                    wait(sp, row_ready, b + 1)
                    sp.dma_start(xrow[bass.ds(b * S, S), :], xr[:, p, :]).then_inc(row_out[p], 16)
                if has(-1):
                    b, p = i - 1, 1 - par
                    wait(sp, h1_ready, b + 1)
                    sp.dma_start(out[bass.ds(b * S, S), :], h1[:, p, :]).then_inc(h1_out[p], 16)
                if has(-3):
                    b, p = i - 3, 1 - par
                    wait(sp, cnt_copied, b + 1)
                    sp.dma_start(counts_dram[bass.ds(b, 1), :, :].rearrange("b e s -> e (b s)"),
                                 cnt[:, p, :]).then_inc(cnt_out[p], 16)

            steps(sp, step)

            for n in range(2):
                sp.wait_ge(cnt_out[n], 16 * NB // 2)
            sp.dma_start(cum[:], counts_dram).then_inc(cum_in, 16)
            sp.dma_start(cum_p[1:NB, :, :], counts_dram[0:NB - 1, :, :]).then_inc(cum_in, 16)

            with sp.Fori(1, NE // 2) as t:
                for p in range(2):
                    load(2 * t + p, p, t)
            for n in range(2):
                sp.wait_ge(added[n], 16 * CC * NE // 2)

        @block.gpsimd
        def _(pool):
            nc.gpsimd.memset(ident[:], 0.0).then_inc(pool_step, 1)
            nc.gpsimd.memset(upper_f[:], 1.0).then_inc(pool_step, 1)
            nc.gpsimd.memset(minus_half[:], -0.5)
            nc.gpsimd.iota(rel_i[:], pattern=[[1, S]], base=0, channel_multiplier=-1)
            nc.gpsimd.iota(part_i[:], pattern=[[0, 1]], base=0, channel_multiplier=1)
            nc.gpsimd.iota(slot_i[:], pattern=[[1, CAP]], base=0, channel_multiplier=0)
            nc.gpsimd.iota(seq_i[:], pattern=[[0, 1]], base=0, channel_multiplier=P)
            nc.gpsimd.iota(slotp_i[:], pattern=[[P, CC]], base=0, channel_multiplier=1)
            pool.wait_ge(pool_step, 2)
            nc.gpsimd.affine_select(out=ident[:], in_=ident[:], compare_op=ALU.not_equal, fill=1.0, base=0,
                                    pattern=[[-1, P]], channel_multiplier=1)
            nc.gpsimd.affine_select(out=upper_f[:], in_=upper_f[:], compare_op=ALU.is_ge, fill=0.0, base=0,
                                    pattern=[[1, P]], channel_multiplier=-1).then_inc(pool_const, 1)

            def prepare_gather(b, p, t):
                wait(pool, embT_done, b - 1)
                wait(pool, gathered[p], 64 * t)
                nc.gpsimd.tensor_copy(idx[:, p, :], ids_all[:, bass.ds(b, 1), :].rearrange("p b n -> p (b n)")
                                      ).then_inc(idx_copied, 1)
                nc.gpsimd.memset(emb[:, p, :], 0.0).then_inc(emb_clear, 1)
                wait(pool, emb_clear, b + 1)
                wait(pool, idx_copied, b + 1)

            def gather(p):
                for n in range(4):
                    nc.gpsimd.indirect_dma_start(
                        out=emb[:, p, STARTS[n]:STARTS[n] + WIDTHS[n]], out_offset=None, in_=EMBS[n],
                        in_offset=bass.IndirectOffsetOnAxis(ap=idx[:, p, n:n + 1], axis=0),
                        bounds_check=EMBS[n].shape[0] - 1, oob_is_err=False).then_inc(gathered[p], 16)

            def step(i, par, has, t):
                if has(3):
                    prepare_gather(i + 3, 1 - par, t(3))
                if has(0):
                    b, p = i, par
                    wait(pool, h_copied, b + 1)
                    wait(pool, h1_ready, b - 1)
                    nc.gpsimd.tensor_tensor(hb[:, p, :], h_all[:, bass.ds(b, 1), :].rearrange("p b n -> p (b n)"),
                                            pbias[:], ALU.add).then_inc(hb_ready, 1)
                if has(3):
                    gather(1 - par)
                if has(2):
                    b, p = i + 2, par
                    wait(pool, var1_ready, b + 1)
                    nc.gpsimd.tensor_tensor(rs1[:, p, :], ve1[:, p, :], minus_half[:], ALU.pow).then_inc(rs1_ready, 1)
                if has(-1):
                    b, p = i - 1, 1 - par
                    wait(pool, var2_ready, b + 1)
                    nc.gpsimd.tensor_tensor(rs2[:, p, :], ve2[:, p, :], minus_half[:], ALU.pow).then_inc(rs2_ready, 1)

            pool.wait_ge(ids_ready, 1)
            for i in range(-AHEAD, FULL_LO):
                if i == 0:
                    pool.wait_ge(weights_in, 64)
                step(i, i % 2, lambda lag, i=i: 0 <= i + lag < NB, lambda lag, i=i: (i + lag) // 2)
            with pool.Fori(FULL_LO // 2, FULL_HI // 2) as t:
                for par in range(2):
                    step(2 * t + par, par, lambda lag: True, lambda lag: t + (par + lag) // 2)
            for i in range(FULL_HI, NB + BEHIND):
                step(i, i % 2, lambda lag, i=i: 0 <= i + lag < NB, lambda lag, i=i: (i + lag) // 2)

            pool.wait_ge(spare_out, 32)
            for n in range(2):
                pool.wait_ge(row_out[n], 16 * NB // 2)
                pool.wait_ge(h1_out[n], 16 * NB // 2)

            def fetch(e, p, t):
                wait(pool, rows_ready, e + 1)
                wait(pool, xg_in[p], 16 * CC * t)
                wait(pool, xgT_done, e - 1)
                wait(pool, wcol_ready, e - 1)
                nc.gpsimd.tensor_copy(gidx[:, p, :], rows_all[:, bass.ds(e, 1), :].rearrange("p e c -> p (e c)")
                                      ).then_inc(gidx_copied, 1)
                pool.wait_ge(spare_out, 32)
                wait(pool, gidx_copied, e + 1)
                for c in range(CC):
                    nc.gpsimd.indirect_dma_start(
                        out=xg[:, p, c, :], out_offset=None, in_=xrow,
                        in_offset=bass.IndirectOffsetOnAxis(ap=gidx[:, p, c:c + 1], axis=0),
                        bounds_check=NTOK + CAP - 1, oob_is_err=False).then_inc(xg_in[p], 16)

            def add(e, p, t):
                if known(e) and e == 0:
                    pass
                else:
                    wait(pool, added[1 - p], 16 * CC * (t + p))
                nc.gpsimd.tensor_copy(sidx[:, p, :], rows_all[:, bass.ds(e, 1), :].rearrange("p e c -> p (e c)")
                                      ).then_inc(sidx_copied, 1)
                pool.wait_ge(spare_out, 32)
                wait(pool, eo_ready, e + 1)
                wait(pool, sidx_copied, e + 1)
                for c in range(CC):
                    nc.gpsimd.indirect_dma_start(
                        out=out, out_offset=bass.IndirectOffsetOnAxis(ap=sidx[:, p, c:c + 1], axis=0),
                        in_=eo[:, p, c, :], in_offset=None, bounds_check=NTOK + CAP - 1, oob_is_err=True,
                        compute_op=ALU.add).then_inc(added[p], 16)

            fetch(0, 0, 0)
            fetch(1, 1, 0)
            for p in range(2):
                fetch(2 + p, p, 1)
                add(p, p, 0)
            with pool.Fori(1, NE // 2 - 1) as t:
                for p in range(2):
                    fetch(2 * t + 2 + p, p, t + 1)
                    add(2 * t + p, p, t)
            for p in range(2):
                add(NE - 2 + p, p, NE // 2 - 1)

        @block.scalar
        def _(act):
            def exps(i, p, c):
                wait(act, min_ready, NC * i + c + 1)
                for j in range(HC):
                    last = nc.scalar.activation(sc[:, p, c, j, :], sc[:, p, c, j, :], ACT.Exp,
                                                bias=mn[:, p, c, j:j + 1], scale=-1.0)
                last.then_inc(prob_ready, 1)

            def probT_copy(i, c):
                wait(act, probT_done, NC * i + c + 1)
                wait(act, pv_done, NC * i + c - 1)
                nc.scalar.copy(pT[:, c % 2, :, :], probT_ps[c % 2][:].rearrange("p (j s) -> p j s", j=HC)
                               ).then_inc(probT_copied, 1)

            def step(i, par, has):
                if has(2):
                    b, p = i + 2, par
                    wait(act, embT_done, b + 1)
                    nc.scalar.copy(embT[:, p, 0:KC * P], embT_ps[:, 0:KC * P])
                    nc.scalar.copy(embT[0:ER, p, KC * P:], embT_ps[0:ER, KC * P:(KC + 1) * P]).then_inc(embT_copied, 1)
                if has(0):
                    exps(i, par, 0)
                if has(-3):
                    b, p = i - 3, 1 - par
                    wait(act, nmax_ready, b + 1)
                    nc.scalar.activation(ex[:, p, :], logits[:, p, :], ACT.Exp, bias=nmax[:, p, :]).then_inc(ex_ready, 1)
                if has(2):
                    b = i + 2
                    wait(act, h_done, b + 1)
                    nc.scalar.copy(h_all[:, bass.ds(b, 1), :].rearrange("p b n -> p (b n)"), h_ps).then_inc(h_copied, 1)
                if has(0):
                    exps(i, par, 1)
                if has(1):
                    b, p = i + 1, 1 - par
                    wait(act, ln1T_done, b + 1)
                    nc.scalar.copy(ln1T[:, p, :], ln1T_ps).then_inc(ln1T_copied, 1)
                if has(0):
                    probT_copy(i, 0)
                if has(-1):
                    b, p = i - 1, 1 - par
                    wait(act, yT_done, b + 1)
                    nc.scalar.copy(yT[:, p, :], yT_ps).then_inc(yT_copied, 1)
                if has(0):
                    exps(i, par, 2)
                    probT_copy(i, 1)
                    exps(i, par, 3)
                    probT_copy(i, 2)
                if has(-2):
                    b, p = i - 2, par
                    wait(act, ln2T_done, b + 1)
                    nc.scalar.copy(ln2T[:, p, :], ln2T_ps).then_inc(ln2T_copied, 1)
                if has(0):
                    probT_copy(i, 3)

            act.wait_ge(zeros_ready, 1)
            nc.scalar.copy(cum_p[0:1, :, :], zeros[0:1, 0, 0:S].unsqueeze(1).to_broadcast([1, NE, S])).then_inc(cum_clear, 1)
            steps(act, step)

            def weights(e, p):
                wait(act, guT_done, e + 1)
                nc.scalar.copy(guT[:, p, 0, :], guT_ps[0][:, 0:F2])
                wait(act, dnT_done, e + 1)
                nc.scalar.copy(dnT[:, p, 0, :], dnT_ps[:, 0:DM])
                nc.scalar.copy(dnT[0:F1, p, 1, :], dnT_ps[0:F1, DM:2 * DM]).then_inc(wT_copied_act, 1)
                wait(act, xgT_done, e + 1)
                nc.scalar.copy(xgT[:, p, :, :], xgT_ps[:].rearrange("p (c s) -> p c s", c=KC)).then_inc(xgT_copied, 1)

            def silus(e):
                wait(act, gate_done, 3 * e + 2)
                wait(act, hT_ready, e)
                nc.scalar.activation(silu_a[:], gate_ps, ACT.Silu)
                nc.scalar.activation(silu_b[:], mixed_ps[0:F1, :], ACT.Silu).then_inc(silu_ready, 1)

            weights(0, 0)
            silus(0)
            for p in range(2):
                weights(1 + p, 1 - p)
                silus(1 + p)
            with act.Fori(1, NE // 2 - 1) as t:
                for p in range(2):
                    weights(2 * t + 1 + p, 1 - p)
                    silus(2 * t + 1 + p)
            weights(NE - 1, 1)
            silus(NE - 1)

        @block.vector
        def _(dve):
            v = nc.vector
            chain = [0]

            def link(ins):
                chain[0] += 1
                ins.then_inc(dve_step, 1)
                dve.wait_ge(dve_step, chain[0])

            dve.wait_ge(ids_in, 16)
            v.tensor_copy(ids_f[:], ids_rows[:]).then_inc(ids_float, 1)
            v.memset(zeros[:], 0.0).then_inc(zeros_ready, 1)
            v.memset(ones[:], 1.0)
            v.memset(seen[:, 1, :], 0.0)
            v.memset(vv[:, :, :, D:D + 1], 1.0)
            dve.wait_ge(pool_const, 1)
            v.tensor_copy(upper[:], upper_f[:])
            link(v.tensor_copy(rel[:], rel_i[:]))
            dve.wait_ge(setup_T, 1)
            link(v.tensor_copy(ids_t[:], bank[3][:, 0:NB]))
            for n in range(4):
                v.tensor_scalar(low[:, n, :], ids_t[:], float(FIRST_ID[n]), BIG, ALU.is_lt, ALU.mult)
                last = v.tensor_scalar(shifted[:, n, :], ids_t[:], -float(FIRST_ID[n]), None, ALU.add)
            link(last)
            v.tensor_tensor(ids_all[:].rearrange("p b n -> p n b"), low[:], shifted[:], ALU.add).then_inc(ids_ready, 1)
            v.tensor_scalar(later[:], rel[:], 0.0, NEG, ALU.is_gt, ALU.mult)
            link(v.tensor_scalar(part_b[:], part_i[:], D, None, ALU.bitwise_and))
            link(v.tensor_scalar(even[:], part_b[:], 0.0, None, ALU.is_equal))
            v.tensor_scalar(odd[:], even[:], -1.0, 1.0, ALU.mult, ALU.add)
            dve.wait_ge(small_in, 16 * 7)
            link(v.tensor_scalar(slopes_n[:], slopes_b[:], -1.0, None, ALU.mult))
            dve.wait_ge(setup_T, 2)
            v.tensor_copy(projT[:], bank[0][:].rearrange("p (c n) -> p c n", c=KC))
            v.tensor_copy(projT_r[:], bank[1][0:ER, 0:DM]).then_inc(proj_ready, 1)
            v.tensor_copy(gateT[:], bank[2][:, 0:KC * NE].rearrange("p (c n) -> p c n", c=KC))
            link(v.tensor_copy(bias_t[:], bank[2][:, 128:128 + 3 * KC]))
            v.tensor_scalar(qbias[:], bias_t[:, KC:2 * KC], QSCALE, None, ALU.mult)
            v.tensor_scalar(kbias_even[:], bias_t[:, 0:KC], even[:], None, ALU.mult)
            v.tensor_scalar(kbias_odd[:], bias_t[:, 0:KC], odd[:], None, ALU.mult)
            for c in range(NC):
                for j in range(HC):
                    n = head_of(c, j)
                    v.scalar_tensor_tensor(bias_neg[:, c, j, :], rel[:], slopes_n[:, n:n + 1], later[:], ALU.mult, ALU.add)
            dve.wait_ge(weights_in, 64)
            v.tensor_scalar(wq[:], wkqv[:, :, DM:2 * DM], QSCALE, None, ALU.mult).then_inc(setup_ready, 1)
            dve.wait_ge(setup_ready, 1)

            def scores(i, p, c):
                n = NC * i + c
                wait(dve, score_done, n + 1)
                if c == 0:
                    wait(dve, pv_done, NC * (i - 1))
                v.tensor_tensor(sc[:, p, c, :, :], score_ps[c % 2][:].rearrange("p (j s) -> p j s", j=HC),
                                bias_neg[:, c, :, :], ALU.add).then_inc(score_read, 1)
                wait(dve, score_read, n + 1)
                v.tensor_reduce(mn[:, p, c, :], sc[:, p, c, :, :], axis=AX.X, op=ALU.min).then_inc(min_ready, 1)

            def variance(st, mv, ve, b, mv_done, var_ready):
                v.bn_aggr(mv, st).then_inc(mv_done, 1)
                wait(dve, mv_done, b + 1)
                v.tensor_scalar(ve, mv[:, 1:2], EPS, None, ALU.add).then_inc(var_ready, 1)

            def step(i, par, has, t):
                if has(0):
                    wait(dve, v_done, i + 1)
                    wait(dve, pv_done, NC * (i - 1))
                    v.tensor_tensor(vv[:, par, :, 0:D], v_ps.rearrange("p (h d) -> p h d", h=H),
                                    vbias[:].rearrange("p (h d) -> p h d", h=H), ALU.add).then_inc(v_ready, 1)
                    scores(i, par, 0)
                if has(-3):
                    b, p = i - 3, 1 - par
                    v.max(top8[:, p, :], logits[:, p, :]).then_inc(top8_ready, 1)
                    wait(dve, top8_ready, b + 1)
                    v.tensor_scalar(nmax[:, p, :], top8[:, p, 0:1], -1.0, None, ALU.mult).then_inc(nmax_ready, 1)
                    v.match_replace(rest[:, p, :], top8[:, p, :], logits[:, p, :], -3e38).then_inc(rest_ready, 1)
                    wait(dve, rest_ready, b + 1)
                    wait(dve, cnt_done, b - 1)
                    v.tensor_tensor(mask[:, p, :], logits[:, p, :], rest[:, p, :], ALU.not_equal).then_inc(mask_ready, 1)
                    wait(dve, mask_ready, b + 1)
                    wait(dve, seen_ready, b)
                    wait(dve, cnt_done, b)
                    v.tensor_tensor(seen[:, p, :], seen[:, 1 - p, :], mask[:, p, :], ALU.add).then_inc(seen_ready, 1)
                if has(0):
                    scores(i, par, 1)
                if has(2):
                    b, p = i + 2, par
                    wait(dve, h_copied, b + 1)
                    v.bn_stats(st1[:, p, :], h_all[:, bass.ds(b, 1), :].rearrange("p b n -> p (b n)")).then_inc(st1_done, 1)
                    wait(dve, st1_done, b + 1)
                if has(-1):
                    b, p = i - 1, 1 - par
                    wait(dve, pv_done, NC * (b + 1))
                    v.reciprocal(rden[:, p, :], y_ps[:, :, D:D + 1].rearrange("p h o -> p (h o)")).then_inc(rden_ready, 1)
                    wait(dve, rden_ready, b + 1)
                    wait(dve, yT_done, b - 1)
                    v.tensor_tensor(y[:, p, :].rearrange("p (h d) -> p h d", h=H), y_ps[:, :, 0:D],
                                    rden[:, p, :].unsqueeze(2).to_broadcast([P, H, D]), ALU.mult).then_inc(y_ready, 1)
                if has(-3):
                    b, p = i - 3, 1 - par
                    wait(dve, ex_ready, b + 1)
                    v.scalar_tensor_tensor(exm[:, p, :], ex[:, p, :], 1.0, mask[:, p, :], ALU.mult, ALU.mult,
                                           accum_out=esum[:, p, :]).then_inc(exm_ready, 1)
                    wait(dve, exm_ready, b + 1)
                    v.reciprocal(rsum[:, p, :], esum[:, p, :]).then_inc(rsum_ready, 1)
                    wait(dve, rsum_ready, b + 1)
                    v.tensor_scalar(xr[:, p, DM:XW], exm[:, p, :], rsum[:, p, :], None, ALU.mult).then_inc(row_ready, 1)
                if has(0):
                    scores(i, par, 2)
                if has(2):
                    b, p = i + 2, par
                    variance(st1[:, p, :], mv1[:, p, :], ve1[:, p, :], b, mv1_done, var1_ready)
                if has(0):
                    scores(i, par, 3)
                if has(1):
                    b, p = i + 1, 1 - par
                    wait(dve, qk_done, b + 1)
                    wait(dve, score_done, NC * (b - 1))
                    v.tensor_tensor(qT[:, p, :, :], q_ps, qbias[:].unsqueeze(2).to_broadcast([P, KC, S]), ALU.add)
                    v.scalar_tensor_tensor(kT[:, p, :, 0, :], k_ps, even[:],
                                           kbias_even[:].unsqueeze(2).to_broadcast([P, KC, S]), ALU.mult, ALU.add)
                    v.scalar_tensor_tensor(kT[:, p, :, 1, :], k_ps, odd[:],
                                           kbias_odd[:].unsqueeze(2).to_broadcast([P, KC, S]), ALU.mult, ALU.add
                                           ).then_inc(qk_ready, 1)
                if has(-1):
                    b, p = i - 1, 1 - par
                    wait(dve, proj_done, b + 1)
                    wait(dve, hb_ready, b + 1)
                    wait(dve, h1_out[p], 16 * t(-1))
                    v.tensor_tensor(h1[:, p, :], proj_ps, hb[:, p, :], ALU.add).then_inc(h1_ready, 1)
                    wait(dve, h1_ready, b + 1)
                    v.bn_stats(st2[:, p, :], h1[:, p, :]).then_inc(st2_done, 1)
                    wait(dve, st2_done, b + 1)
                if has(2):
                    b, p = i + 2, par
                    wait(dve, rs1_ready, b + 1)
                    wait(dve, ln1T_done, b - 1)
                    v.tensor_scalar(ln1[:, p, :], h_all[:, bass.ds(b, 1), :].rearrange("p b n -> p (b n)"),
                                    mv1[:, p, 0:1], rs1[:, p, :], ALU.subtract, ALU.mult).then_inc(ln1_ready, 1)
                if has(-1):
                    b, p = i - 1, 1 - par
                    variance(st2[:, p, :], mv2[:, p, :], ve2[:, p, :], b, mv2_done, var2_ready)
                if has(-2):
                    b, p = i - 2, par
                    wait(dve, logit_done, b + 1)
                    v.tensor_copy(logits[:, p, :], logit_ps).then_inc(logit_copied, 1)
                    wait(dve, logit_copied, b + 1)
                if has(-3):
                    b, p = i - 3, 1 - par
                    wait(dve, cnt_done, b + 1)
                    wait(dve, cnt_out[p], 16 * t(-3))
                    v.tensor_scalar(cnt[:, p, :], cnt_ps, float(CAP), None, ALU.min).then_inc(cnt_copied, 1)
                if has(-1):
                    b, p = i - 1, 1 - par
                    wait(dve, rs2_ready, b + 1)
                    wait(dve, row_out[p], 16 * t(-1))
                    v.tensor_scalar(xr[:, p, 0:DM], h1[:, p, :], mv2[:, p, 0:1], rs2[:, p, :],
                                    ALU.subtract, ALU.mult).then_inc(ln2_ready, 1)

            for i in range(-AHEAD, FULL_LO):
                step(i, i % 2, lambda lag, i=i: 0 <= i + lag < NB, lambda lag, i=i: (i + lag) // 2)
            with dve.Fori(FULL_LO // 2, FULL_HI // 2) as t:
                for par in range(2):
                    step(2 * t + par, par, lambda lag: True, lambda lag: t + (par + lag) // 2)
            for i in range(FULL_HI, NB + BEHIND):
                step(i, i % 2, lambda lag, i=i: 0 <= i + lag < NB, lambda lag, i=i: (i + lag) // 2)

            def weights(e, p):
                wait(dve, guT_done, e + 1)
                v.tensor_copy(guT[:, p, 1, :], guT_ps[1][:, 0:F2]).then_inc(wT_copied_dve, 1)

            v.tensor_copy(slot_row[:], slot_i[:])
            v.memset(seq_col[:, 1:2], 1.0)
            v.tensor_copy(seq_col[:, 0:1], seq_i[:])
            v.tensor_copy(slotp[:], slotp_i[:])
            v.tensor_scalar(spare[:], slotp_i[:], float(NTOK - P), None, ALU.add).then_inc(slots_ready, 1)
            dve.wait_ge(slots_ready, 1)
            weights(0, 0)
            dve.wait_ge(cum_in, 32)

            def spread(e, p):
                wait(dve, onehot_ready, e - 1)
                v.tensor_scalar(before[:, p, :], slot_row[:], cum_p[:, bass.ds(e, 1), S - 1:S].rearrange("b e s -> b (e s)"),
                                None, ALU.is_lt).then_inc(before_ready, 1)
                wait(dve, before_ready, e + 1)
                wait(dve, rows_done, e - 1)
                v.scalar_tensor_tensor(onehot[:, p, :], slot_row[:],
                                       cum[:, bass.ds(e, 1), S - 1:S].rearrange("b e s -> b (e s)"),
                                       before[:, p, :], ALU.is_lt, ALU.subtract).then_inc(onehot_ready, 1)

            def number(e, p):
                wait(dve, rows_done, e + 1)
                for c in range(CC):
                    v.tensor_scalar(le[:, p, c, :], cumrow_ps[:, c, :], slotp[:, c:c + 1], None, ALU.is_le, ALU.add,
                                    accum_out=nle[:, p, c:c + 1])
                v.tensor_tensor(t_a[:, p, :], base_ps[:, :, 1], spare[:], ALU.mult).then_inc(row_a, 1)
                wait(dve, row_a, e + 1)
                v.tensor_tensor(t_b[:, p, :], spare[:], t_a[:, p, :], ALU.subtract).then_inc(row_b, 1)
                v.tensor_tensor(t_c[:, p, :], base_ps[:, :, 0], nle[:, p, :], ALU.add).then_inc(row_c, 1)
                wait(dve, row_b, e + 1)
                wait(dve, row_c, e + 1)
                v.tensor_tensor(rows_all[:, bass.ds(e, 1), :].rearrange("p e c -> p (e c)"), t_b[:, p, :], t_c[:, p, :],
                                ALU.add).then_inc(rows_ready, 1)

            def take_weights(e, p, t):
                wait(dve, xg_in[p], 16 * CC * (t + 1))
                wait(dve, eo_ready, e - 1)
                v.tensor_copy(wcol[:, p, :], xg[:, p, :, bass.ds(e + DM, 1)].rearrange("p c o -> p (c o)")
                              ).then_inc(wcol_ready, 1)

            def gates(e):
                wait(dve, silu_ready, e + 1)
                wait(dve, gate_done, 3 * e + 3)
                wait(dve, eo_done, e)
                v.tensor_tensor(hT_a[:], silu_a[:], up_ps, ALU.mult)
                v.tensor_tensor(hT_b[:], silu_b[:], mixed_ps[F1:P, :], ALU.mult).then_inc(hT_ready, 1)

            def weigh(e, p, t):
                wait(dve, eo_done, e + 1)
                wait(dve, wcol_ready, e + 1)
                wait(dve, added[p], 16 * CC * t)
                for c in range(CC):
                    last = v.tensor_scalar(eo[:, p, c, :], eo_ps[:, c * DM:(c + 1) * DM], wcol[:, p, c:c + 1], None,
                                           ALU.mult)
                last.then_inc(eo_ready, 1)

            spread(0, 0)
            number(0, 0)
            spread(1, 1)
            number(1, 1)
            take_weights(0, 0, 0)

            def expert(e, p, t, ids, more):
                if ids:
                    spread(e + 2, p)
                gates(e)
                if ids:
                    number(e + 2, p)
                if more:
                    weights(e + 1, 1 - p)
                    take_weights(e + 1, 1 - p, t + p)
                weigh(e, p, t)

            for p in range(2):
                expert(p, p, 0, True, True)
            with dve.Fori(1, NE // 2 - 1) as t:
                for p in range(2):
                    expert(2 * t + p, p, t, True, True)
            expert(NE - 2, 0, NE // 2 - 1, False, True)
            expert(NE - 1, 1, NE // 2 - 1, False, False)

        @block.tensor
        def _(pe):
            mm, tr = nc.tensor.matmul, nc.tensor.transpose
            pe.wait_ge(pool_const, 1)
            pe.wait_ge(ids_float, 1)
            tr(bank[3][:, 0:NB], ids_f[:], ident[0:NB, 0:NB]).then_inc(setup_T, 1)
            pe.wait_ge(small_in, 16 * 7)
            for c in range(KC):
                for r in range(KC):
                    tr(bank[0][:, c * DM + r * P:c * DM + (r + 1) * P], proj_rows[:, r, c * P:(c + 1) * P], ident[:])
            for r in range(KC):
                tr(bank[1][0:ER, r * P:(r + 1) * P], proj_rows[:, r, KC * P:EW], ident[:])
                tr(bank[2][:, r * NE:(r + 1) * NE], gate_rows[:, r * P:(r + 1) * P], ident[0:NE, 0:NE])
            tr(bank[2][:, 128:128 + 3 * KC], bias_rows[:], ident[0:3 * KC, 0:3 * KC]).then_inc(setup_T, 1)
            pe.wait_ge(proj_ready, 1)

            def transposed(dst, src, done):
                for c in range(KC):
                    last = tr(dst[:, c * P:(c + 1) * P], src[:, c * P:(c + 1) * P], ident[:])
                last.then_inc(done, 1)

            def score(i, p, c):
                n = NC * i + c
                if c == 0:
                    wait(pe, qk_ready, i + 1)
                wait(pe, score_read, n - 1)
                if c == 1:
                    wait(pe, v_ready, i + 1)
                rows = slice(2 * D * c, 2 * D * (c + 1))
                for r in range(KC):
                    last = mm(score_ps[c % 2][:, r * 2 * S:(r + 1) * 2 * S], qT[rows, p, r, :],
                              kT[rows, p, r, :, :].rearrange("p a s -> p (a s)"), start=True, stop=True)
                last.then_inc(score_done, 1)

            def probT(i, p, c):
                n = NC * i + c
                wait(pe, prob_ready, n + 1)
                wait(pe, probT_copied, n - 1)
                for j in range(HC):
                    last = tr(probT_ps[c % 2][:, j * S:(j + 1) * S], sc[:, p, c, j, :], ident[:])
                last.then_inc(probT_done, 1)

            def pv(i, p, c):
                if c == 0:
                    wait(pe, v_ready, i + 1)
                    wait(pe, y_ready, i)
                wait(pe, probT_copied, NC * i + c + 1)
                for j in range(HC):
                    n = head_of(c, j)
                    last = mm(y_ps[:, n, :], pT[:, c % 2, j, :], vv[:, p, n, :], start=True, stop=True)
                last.then_inc(pv_done, 1)

            def qk(i, par, n, w):
                b, p = i + 1, 1 - par
                if n == 0:
                    wait(pe, ln1T_copied, b + 1)
                    wait(pe, score_read, NC * b - 1)
                for r in range(KC):
                    o = (n * KC + r) * S
                    for c in range(KC):
                        last = mm(bank[0][:, o:o + S], w[:, c, r * P:(r + 1) * P],
                                  ln1T[:, p, c * P:(c + 1) * P], start=(c == 0), stop=(c == KC - 1))
                if n == 1:
                    last.then_inc(qk_done, 1)

            def step(i, par, has, t):
                if has(0):
                    wait(pe, ln1T_copied, i + 1)
                    wait(pe, score_read, NC * i)
                    for c in range(KC):
                        last = mm(v_ps, ln1T[:, par, c * P:(c + 1) * P], wkqv[:, c, 2 * DM:3 * DM],
                                  start=(c == 0), stop=(c == KC - 1))
                    last.then_inc(v_done, 1)
                    score(i, par, 0)
                if has(2):
                    b, p = i + 2, par
                    wait(pe, gathered[p], 64 * (t(2) + 1))
                    wait(pe, h_copied, b)
                    wait(pe, ln2T_copied, b - 4)
                    for c in range(KC):
                        tr(embT_ps[:, c * P:(c + 1) * P], emb[:, p, c * P:(c + 1) * P], ident[:])
                    tr(embT_ps[0:ER, KC * P:(KC + 1) * P], emb[:, p, KC * P:EW], ident[:]).then_inc(embT_done, 1)
                if has(-1):
                    pv(i - 1, 1 - par, 2)
                if has(0):
                    score(i, par, 1)
                if has(2):
                    b, p = i + 2, par
                    wait(pe, embT_copied, b + 1)
                    for c in range(KC):
                        mm(h_ps, embT[:, p, c * P:(c + 1) * P], projT[:, c, :], start=(c == 0), stop=False)
                    mm(h_ps, embT[0:ER, p, KC * P:(KC + 1) * P], projT_r[:], start=False, stop=True).then_inc(h_done, 1)
                if has(-1):
                    pv(i - 1, 1 - par, 3)
                if has(0):
                    score(i, par, 2)
                if has(1):
                    b, p = i + 1, 1 - par
                    wait(pe, ln1_ready, b + 1)
                    wait(pe, yT_copied, b - 2)
                    transposed(ln1T_ps, ln1[:, p, :], ln1T_done)
                if has(0):
                    probT(i, par, 0)
                if has(-1):
                    b, p = i - 1, 1 - par
                    wait(pe, y_ready, b + 1)
                    wait(pe, ln1T_copied, min(b + 3, NB) if known(b) else b + 3)
                    transposed(yT_ps, y[:, p, :], yT_done)
                if has(0):
                    score(i, par, 3)
                if has(1):
                    qk(i, par, 0, wq)
                if has(0):
                    probT(i, par, 1)
                if has(1):
                    qk(i, par, 1, wkqv)
                if has(0):
                    pv(i, par, 0)
                    probT(i, par, 2)
                if has(-1):
                    b, p = i - 1, 1 - par
                    wait(pe, yT_copied, b + 1)
                    wait(pe, h1_ready, b)
                    wait(pe, logit_copied, b - 1)
                    wait(pe, cnt_copied, b - 2)
                    for c in range(KC):
                        last = mm(proj_ps, yT[:, p, c * P:(c + 1) * P], wproj[:, c, :], start=(c == 0), stop=(c == KC - 1))
                    last.then_inc(proj_done, 1)
                if has(0):
                    pv(i, par, 1)
                if has(-2):
                    b, p = i - 2, par
                    wait(pe, ln2_ready, b + 1)
                    wait(pe, h_copied, NB if known(b) and b + 5 > NB else b + 5)
                    transposed(ln2T_ps, xr[:, p, 0:DM], ln2T_done)
                if has(0):
                    probT(i, par, 3)
                if has(-3):
                    b, p = i - 3, 1 - par
                    wait(pe, seen_ready, b + 1)
                    wait(pe, cnt_copied, b)
                    wait(pe, logit_copied, b + 1)
                    wait(pe, h1_ready, min(b + 3, NB) if known(b) else b + 3)
                    mm(cnt_ps, mask[:, p, :], upper[:], start=True, stop=False)
                    mm(cnt_ps, seen[:, 1 - p, :], ones[:], start=False, stop=True).then_inc(cnt_done, 1)
                if has(-2):
                    b, p = i - 2, par
                    wait(pe, ln2T_copied, b + 1)
                    wait(pe, logit_copied, b)
                    wait(pe, cnt_copied, b - 1)
                    wait(pe, h1_ready, min(b + 2, NB) if known(b) else b + 2)
                    for c in range(KC):
                        last = mm(logit_ps, ln2T[:, p, c * P:(c + 1) * P], gateT[:, c, :], start=(c == 0), stop=(c == KC - 1))
                    last.then_inc(logit_done, 1)

            for i in range(-AHEAD, FULL_LO):
                if i == -1:
                    pe.wait_ge(setup_ready, 1)
                step(i, i % 2, lambda lag, i=i: 0 <= i + lag < NB, lambda lag, i=i: (i + lag) // 2)
            with pe.Fori(FULL_LO // 2, FULL_HI // 2) as t:
                for par in range(2):
                    step(2 * t + par, par, lambda lag: True, lambda lag: t + (par + lag) // 2)
            for i in range(FULL_HI, NB + BEHIND):
                step(i, i % 2, lambda lag, i=i: 0 <= i + lag < NB, lambda lag, i=i: (i + lag) // 2)

            pe.wait_ge(cnt_copied, NB)

            def rows(e, p):
                wait(pe, onehot_ready, e + 1)
                wait(pe, rows_ready, e)
                wait(pe, hT_ready, e - 1)
                for c in range(CC):
                    mm(cumrow_ps[:, c, :], onehot[:, p, c * P:(c + 1) * P],
                       cum[:, bass.ds(e, 1), :].rearrange("b e s -> b (e s)"), start=True, stop=True)
                for c in range(CC):
                    last = mm(base_ps[:, c, :], onehot[:, p, c * P:(c + 1) * P], seq_col[:], start=True, stop=True)
                last.then_inc(rows_done, 1)

            def weightsT(e, p, t):
                wait(pe, gu_in[p], 48 * (t + 1))
                wait(pe, wT_copied_act, e)
                wait(pe, wT_copied_dve, e)
                for c in range(KC):
                    for m in range(F2 // P):
                        last = tr(guT_ps[c][:, m * P:(m + 1) * P], gu[:, p, m, c * P:(c + 1) * P], ident[:])
                last.then_inc(guT_done, 1)
                wait(pe, dn_in[p], 16 * (t + 1))
                for c in range(KC):
                    tr(dnT_ps[:, c * P:(c + 1) * P], dn[:, p, c, 0:P], ident[:])
                    last = tr(dnT_ps[0:F1, DM + c * P:DM + (c + 1) * P], dn[:, p, c, P:F], ident[:])
                last.then_inc(dnT_done, 1)

            def tokensT(e, p, t):
                wait(pe, xg_in[p], 16 * CC * (t + 1))
                for k in range(KC):
                    for c in range(CC):
                        last = tr(xgT_ps[:, k * CAP + c * P:k * CAP + (c + 1) * P], xg[:, p, c, k * P:(k + 1) * P], ident[:])
                last.then_inc(xgT_done, 1)

            def gate_up(e, p):
                wait(pe, wT_copied_act, e + 1)
                wait(pe, wT_copied_dve, e + 1)
                wait(pe, xgT_copied, e + 1)
                wait(pe, hT_ready, e)
                wait(pe, rows_ready, min(e + 2, NE) if known(e) else e + 2)
                for m, dst in enumerate((gate_ps, mixed_ps, up_ps)):
                    for k in range(KC):
                        last = mm(dst, guT[:, p, k, m * P:(m + 1) * P], xgT[:, p, k, :], start=(k == 0), stop=(k == KC - 1))
                    last.then_inc(gate_done, 1)

            def down(e, p):
                wait(pe, hT_ready, e + 1)
                wait(pe, eo_ready, e)
                for c in range(CC):
                    cs = slice(c * P, (c + 1) * P)
                    o = eo_ps[:, c * DM:(c + 1) * DM]
                    mm(o, hT_a[:, cs], dnT[:, p, 0, :], start=True, stop=False)
                    last = mm(o, hT_b[:, cs], dnT[0:F1, p, 1, :], start=False, stop=True)
                last.then_inc(eo_done, 1)

            weightsT(0, 0, 0)
            pe.wait_ge(cum_in, 32)
            rows(0, 0)
            rows(1, 1)
            tokensT(0, 0, 0)

            def expert(e, p, t, ids, more):
                gate_up(e, p)
                if more:
                    weightsT(e + 1, 1 - p, t + p)
                if ids:
                    rows(e + 2, p)
                if more:
                    tokensT(e + 1, 1 - p, t + p)
                down(e, p)

            for p in range(2):
                expert(p, p, 0, True, True)
            with pe.Fori(1, NE // 2 - 1) as t:
                for p in range(2):
                    expert(2 * t + p, p, t, True, True)
            expert(NE - 2, 0, NE // 2 - 1, False, True)
            expert(NE - 1, 1, NE // 2 - 1, False, False)


_INS = ['x', 'L0_tok_emb0', 'L0_tok_emb1', 'L0_tok_emb2', 'L0_tok_emb3', 'L0_tok_proj0', 'L0_tok_proj1', 'L0_tok_proj2',
        'L0_tok_proj3', 'L0_attn_W_kqv', 'L0_attn_b_kqv', 'L0_attn_W_proj', 'L0_attn_b_proj', 'L0_attn_slopes',
        'L0_ffn_gate_weight', 'L0_ffn_gate_up_proj', 'L0_ffn_down_proj']
_SPARE = 256


def kernel(**inputs):
    import numpy as _np
    import concourse.bacc as _bacc
    from concourse import mybir as _mybir
    from concourse.bass_utils import run_bass_kernel_spmd as _run

    nc = _bacc.Bacc("TRN2", target_bir_lowering=False, num_devices=1)
    arrays, args = {}, []
    for name in _INS:
        a = _np.ascontiguousarray(inputs[name])
        arrays[f"in_{name}_dram"] = a
        args.append(nc.dram_tensor(f"in_{name}_dram", a.shape, _mybir.dt.from_np(a.dtype), kind="ExternalInput").ap())
    nb, s = inputs['x'].shape
    dm = inputs['L0_tok_emb0'].shape[1]
    args.append(nc.dram_tensor("out_0_dram", (nb * s + _SPARE, dm), _mybir.dt.float32, kind="ExternalOutput").ap())
    bass_lm_tower_kernel(nc, *args)
    r = _run(nc, [arrays], core_ids=[0])
    return r.results[0]["out_0_dram"][0:nb * s].reshape(nb, s, dm)
```

```python
import concourse.bass as bass
from concourse import mybir
from contextlib import ExitStack


def bass_lm_tower_kernel(
    nc: bass.Bass,
    tokens: bass.AP,
    emb0: bass.AP,
    emb1: bass.AP,
    emb2: bass.AP,
    emb3: bass.AP,
    proj0: bass.AP,
    proj1: bass.AP,
    proj2: bass.AP,
    proj3: bass.AP,
    w_kqv: bass.AP,
    b_kqv: bass.AP,
    w_proj: bass.AP,
    b_proj: bass.AP,
    slopes: bass.AP,
    gate_weight: bass.AP,
    gate_up_proj: bass.AP,
    down_proj: bass.AP,
    out: bass.AP,
):
    fp32, bf16, i32 = mybir.dt.float32, mybir.dt.bfloat16, mybir.dt.int32
    fp32r = mybir.dt.float32r
    ALU = mybir.AluOpType
    ACT = mybir.ActivationFunctionType
    AX = mybir.AxisListType

    P = 128
    NB, S = tokens.shape
    DM = emb0.shape[1]
    KC = DM // P
    NTOK = NB * S
    EMBS = [emb0, emb1, emb2, emb3]
    PROJS = [proj0, proj1, proj2, proj3]
    WIDTHS = [e.shape[1] for e in EMBS]
    STARTS = [sum(WIDTHS[:n]) for n in range(4)]
    FIRST_ID = [sum(e.shape[0] for e in EMBS[:n]) for n in range(4)]
    EW = sum(WIDTHS)
    ER = EW - KC * P
    H = slopes.shape[0]
    D = DM // H
    NC = 4
    HC = H // NC
    PAIRS = P // (2 * D)
    NE, F2, _ = gate_up_proj.shape
    F = F2 // 2
    F1 = F - P
    CAP = 256
    CC = CAP // P
    XW = DM + NE
    NEG = 1e30
    BIG = float(1 << 24)
    EPS = 1e-5
    QSCALE = -float(D) ** -0.5

    def head_of(c, j):
        return (j // 2) * 2 * PAIRS + 2 * c + j % 2

    xrow = nc.dram_tensor("xrow", (NTOK + CAP, XW), fp32).ap()
    counts_dram = nc.dram_tensor("counts_dram", (NB - 1, NE, S), bf16).ap()

    ctx = ExitStack()
    with ctx:
        def sb(name, shape, dt=fp32):
            return ctx.enter_context(nc.sbuf_tensor(name, shape, dt))

        def pb(name, shape, dt=fp32):
            return ctx.enter_context(nc.psum_tensor(name, shape, dt))

        def sem(name):
            return ctx.enter_context(nc.semaphore(name))

        ident = sb("ident", [P, P])
        upper_f = sb("upper_f", [P, P])
        upper = sb("upper", [P, P], bf16)
        ones = sb("ones", [P, P], bf16)
        rel_i = sb("rel_i", [P, S], i32)
        rel = sb("rel", [P, S])
        later = sb("later", [P, S])
        bias_neg = sb("bias_neg", [P, NC, HC, S])
        slopes_b = sb("slopes_b", [P, H])
        slopes_n = sb("slopes_n", [P, H])
        minus_half = sb("minus_half", [P, 1])
        part_i = sb("part_i", [P, 1], i32)
        part_b = sb("part_b", [P, 1], i32)
        even = sb("even", [P, 1])
        odd = sb("odd", [P, 1])
        ids_rows = sb("ids_rows", [NB, S], i32)
        ids_f = sb("ids_f", [NB, S])
        ids_t = sb("ids_t", [P, NB])
        low = sb("low", [P, 4, NB])
        shifted = sb("shifted", [P, 4, NB])
        ids_all = sb("ids_all", [P, NB, 4], i32)
        proj_rows = sb("proj_rows", [P, KC, EW])
        projT = sb("projT", [P, KC, DM])
        projT_r = sb("projT_r", [ER, DM])
        gate_rows = sb("gate_rows", [NE, DM])
        gateT = sb("gateT", [P, KC, NE])
        bias_rows = sb("bias_rows", [3 * KC, P])
        bias_t = sb("bias_t", [P, 3 * KC])
        qbias = sb("qbias", [P, KC])
        kbias_even = sb("kbias_even", [P, KC])
        kbias_odd = sb("kbias_odd", [P, KC])
        vbias = sb("vbias", [P, DM])
        pbias = sb("pbias", [P, DM])
        wkqv = sb("wkqv", [P, KC, 3 * DM])
        wq = sb("wq", [P, KC, DM])
        wproj = sb("wproj", [P, KC, DM])
        zeros = sb("zeros", [P, CC, XW])

        idx = sb("idx", [P, 2, 4], i32)
        emb = sb("emb", [P, 2, EW])
        embT = sb("embT", [P, 2, (KC + 1) * P])
        h_all = sb("h_all", [P, NB, DM])
        hb = sb("hb", [P, 2, DM])
        st1 = sb("st1", [P, 2, 6])
        mv1 = sb("mv1", [P, 2, 2])
        ve1 = sb("ve1", [P, 2, 1])
        rs1 = sb("rs1", [P, 2, 1])
        ln1 = sb("ln1", [P, 2, DM])
        ln1T = sb("ln1T", [P, 2, DM])
        qT = sb("qT", [P, 2, KC, S])
        kT = sb("kT", [P, 2, KC, 2, S])
        q_hi = sb("q_hi", [P, 2, KC, S], fp32r)
        q_lo = sb("q_lo", [P, 2, KC, S], fp32r)
        k_hi = sb("k_hi", [P, 2, KC, 2, S], fp32r)
        k_lo = sb("k_lo", [P, 2, KC, 2, S], fp32r)
        vv = sb("vv", [P, 2, H, D + 1])
        sc = sb("sc", [P, 2, NC, HC, S])
        mn = sb("mn", [P, 2, NC, HC])
        pT = sb("pT", [P, 2, HC, S])
        rden = sb("rden", [P, 2, H])
        y = sb("y", [P, 2, DM])
        yT = sb("yT", [P, 2, DM])
        h1 = sb("h1", [P, 2, DM])
        st2 = sb("st2", [P, 2, 6])
        mv2 = sb("mv2", [P, 2, 2])
        ve2 = sb("ve2", [P, 2, 1])
        rs2 = sb("rs2", [P, 2, 1])
        xr = sb("xr", [P, 2, XW])
        ln2T = sb("ln2T", [P, 2, DM])
        logits = sb("logits", [P, 2, NE])
        top8 = sb("top8", [P, 2, 8])
        nmax = sb("nmax", [P, 2, 1])
        rest = sb("rest", [P, 2, NE])
        ex = sb("ex", [P, 2, NE])
        mask = sb("mask", [P, 2, NE], bf16)
        seen = sb("seen", [P, 2, NE], bf16)
        exm = sb("exm", [P, 2, NE])
        esum = sb("esum", [P, 2, 1])
        rsum = sb("rsum", [P, 2, 1])
        cnt = sb("cnt", [NE, 2, S], bf16)

        cum = sb("cum", [NB, NE, S], bf16)
        cum_p = sb("cum_p", [NB, NE, S], bf16)
        slot_i = sb("slot_i", [NB, CAP], i32)
        slot_row = sb("slot_row", [NB, CAP])
        seq_i = sb("seq_i", [NB, 1], i32)
        seq_col = sb("seq_col", [NB, 2], bf16)
        slotp_i = sb("slotp_i", [P, CC], i32)
        slotp = sb("slotp", [P, CC])
        spare = sb("spare", [P, CC])
        before = sb("before", [NB, 2, CAP])
        onehot = sb("onehot", [NB, 2, CAP], bf16)
        le = sb("le", [P, 2, CC, S])
        nle = sb("nle", [P, 2, CC])
        t_a = sb("t_a", [P, 2, CC])
        t_b = sb("t_b", [P, 2, CC])
        t_c = sb("t_c", [P, 2, CC])
        rows_all = sb("rows_all", [P, NE, CC], i32)
        gidx = sb("gidx", [P, 2, CC], i32)
        sidx = sb("sidx", [P, 2, CC], i32)
        xg = sb("xg", [P, 2, CC, XW])
        xgT_hi = sb("xgT_hi", [P, 2, KC, CAP], fp32r)
        xgT_lo = sb("xgT_lo", [P, 2, KC, CAP], fp32r)
        guT_hi = sb("guT_hi", [P, 2, KC, F2], fp32r)
        guT_lo = sb("guT_lo", [P, 2, KC, F2], fp32r)
        wcol = sb("wcol", [P, 2, CC])
        gu = sb("gu", [P, 2, F2 // P, DM])
        dn = sb("dn", [P, 2, KC, F])
        dnT = sb("dnT", [P, 2, 2, DM])
        silu_a = sb("silu_a", [P, CAP])
        silu_b = sb("silu_b", [F1, CAP])
        hT_a = sb("hT_a", [P, CAP])
        hT_b = sb("hT_b", [F1, CAP])
        eo = sb("eo", [P, 2, CC, DM])

        bank = [pb(f"bank{n}", [P, 512]) for n in range(8)]
        score_ps = bank[0:2]
        q_ps = bank[0][:, 0:KC * S].rearrange("p (c s) -> p c s", c=KC)
        k_ps = bank[0][:, KC * S:2 * KC * S].rearrange("p (c s) -> p c s", c=KC)
        v_ps = bank[1][:, 0:DM]
        probT_ps = bank[2:4]
        embT_ps, h_ps, ln2T_ps = bank[4], bank[4][:, 0:DM], bank[4][:, 0:DM]
        yT_ps, ln1T_ps = bank[5][:, 0:DM], bank[5][:, 0:DM]
        proj_ps = bank[6][:, 0:DM]
        logit_ps = bank[6][:, 256:256 + NE]
        cnt_ps = bank[6][0:NE, 384:384 + S]
        y_ps = bank[7][:, 0:H * (D + 1)].rearrange("p (h d) -> p h d", h=H)
        gate_ps, mixed_ps, up_ps = bank[0][:, 0:CAP], bank[1][:, 0:CAP], bank[2][:, 0:CAP]
        cumrow_ps = bank[2][:, CAP:CAP + CC * S].rearrange("p (c s) -> p c s", c=CC)
        base_ps = bank[1][:, CAP:CAP + 2 * CC].rearrange("p (c k) -> p c k", c=CC)
        eo_ps = bank[3]
        guT_ps = bank[4:6]
        dnT_ps = bank[6]
        xgT_ps = bank[7]

        weights_in = sem("weights_in")
        ids_in = sem("ids_in")
        small_in = sem("small_in")
        pool_const = sem("pool_const")
        pool_step = sem("pool_step")
        ids_float = sem("ids_float")
        setup_T = sem("setup_T")
        dve_step = sem("dve_step")
        ids_ready = sem("ids_ready")
        proj_ready = sem("proj_ready")
        setup_ready = sem("setup_ready")
        zeros_ready = sem("zeros_ready")
        spare_out = sem("spare_out")
        emb_clear = sem("emb_clear")
        idx_copied = sem("idx_copied")
        gathered = [sem(f"gathered{n}") for n in range(2)]
        embT_done = sem("embT_done")
        embT_copied = sem("embT_copied")
        h_done = sem("h_done")
        h_copied = sem("h_copied")
        st1_done = sem("st1_done")
        mv1_done = sem("mv1_done")
        var1_ready = sem("var1_ready")
        rs1_ready = sem("rs1_ready")
        hb_ready = sem("hb_ready")
        ln1_ready = sem("ln1_ready")
        ln1T_done = sem("ln1T_done")
        ln1T_copied = sem("ln1T_copied")
        qk_done = sem("qk_done")
        qk_ready = sem("qk_ready")
        qk_hi_ready = sem("qk_hi_ready")
        q_lo_ready = sem("q_lo_ready")
        k_lo_ready = sem("k_lo_ready")
        v_done = sem("v_done")
        v_ready = sem("v_ready")
        score_done = sem("score_done")
        score_read = sem("score_read")
        min_ready = sem("min_ready")
        prob_ready = sem("prob_ready")
        probT_done = sem("probT_done")
        probT_copied = sem("probT_copied")
        pv_done = sem("pv_done")
        rden_ready = sem("rden_ready")
        y_ready = sem("y_ready")
        yT_done = sem("yT_done")
        yT_copied = sem("yT_copied")
        proj_done = sem("proj_done")
        h1_ready = sem("h1_ready")
        st2_done = sem("st2_done")
        mv2_done = sem("mv2_done")
        var2_ready = sem("var2_ready")
        rs2_ready = sem("rs2_ready")
        ln2_ready = sem("ln2_ready")
        ln2T_done = sem("ln2T_done")
        ln2T_copied = sem("ln2T_copied")
        logit_done = sem("logit_done")
        logit_copied = sem("logit_copied")
        top8_ready = sem("top8_ready")
        nmax_ready = sem("nmax_ready")
        rest_ready = sem("rest_ready")
        mask_ready = sem("mask_ready")
        seen_ready = sem("seen_ready")
        ex_ready = sem("ex_ready")
        exm_ready = sem("exm_ready")
        rsum_ready = sem("rsum_ready")
        row_ready = sem("row_ready")
        cnt_done = sem("cnt_done")
        cnt_copied = sem("cnt_copied")
        h1_out = [sem(f"h1_out{n}") for n in range(2)]
        row_out = [sem(f"row_out{n}") for n in range(2)]
        cnt_out = [sem(f"cnt_out{n}") for n in range(2)]
        cum_in = sem("cum_in")
        cum_clear = sem("cum_clear")
        slots_ready = sem("slots_ready")
        before_ready = sem("before_ready")
        onehot_ready = sem("onehot_ready")
        rows_done = sem("rows_done")
        row_a = sem("row_a")
        row_b = sem("row_b")
        row_c = sem("row_c")
        rows_ready = sem("rows_ready")
        gidx_copied = sem("gidx_copied")
        sidx_copied = sem("sidx_copied")
        xg_in = [sem(f"xg_in{n}") for n in range(2)]
        gu_in = [sem(f"gu_in{n}") for n in range(2)]
        dn_in = [sem(f"dn_in{n}") for n in range(2)]
        guT_done = sem("guT_done")
        dnT_done = sem("dnT_done")
        guT_copied = sem("guT_copied")
        dnT_copied = sem("dnT_copied")
        xgT_done = sem("xgT_done")
        guT_rounded = sem("guT_rounded")
        xgT_rounded = sem("xgT_rounded")
        xgT_copied = sem("xgT_copied")
        wcol_ready = sem("wcol_ready")
        gate_done = sem("gate_done")
        silu_ready = sem("silu_ready")
        hT_ready = sem("hT_ready")
        eo_done = sem("eo_done")
        eo_ready = sem("eo_ready")
        added = [sem(f"added{n}") for n in range(2)]

        block = ctx.enter_context(nc.Block())

        AHEAD, BEHIND = 3, 3
        FULL_LO, FULL_HI = BEHIND + 3, NB - AHEAD - 1

        def steps(eng, step):
            for i in range(-AHEAD, FULL_LO):
                step(i, i % 2, lambda lag, i=i: 0 <= i + lag < NB)
            with eng.Fori(FULL_LO // 2, FULL_HI // 2) as t:
                for par in range(2):
                    step(2 * t + par, par, lambda lag: True)
            for i in range(FULL_HI, NB + BEHIND):
                step(i, i % 2, lambda lag, i=i: 0 <= i + lag < NB)

        def known(v):
            return isinstance(v, int)

        def wait(eng, s, v):
            if not known(v) or v > 0:
                eng.wait_ge(s, v)

        @block.sync
        def _(sp):
            sp.dma_start(ids_rows[:], tokens).then_inc(ids_in, 16)
            for n in range(4):
                sp.dma_start(proj_rows[:, :, STARTS[n]:STARTS[n] + WIDTHS[n]],
                             PROJS[n].rearrange("(c p) d -> p c d", p=P)).then_inc(small_in, 16)
            sp.dma_start(gate_rows[:], gate_weight).then_inc(small_in, 16)
            sp.dma_start(bias_rows[:], b_kqv.rearrange("(c p) -> c p", p=P)).then_inc(small_in, 16)
            sp.dma_start(slopes_b[:], slopes.partition_broadcast(P)).then_inc(small_in, 16)
            sp.dma_start(wkqv[:], w_kqv.rearrange("(c p) n -> p c n", p=P)).then_inc(weights_in, 16)
            sp.dma_start(wproj[:], w_proj.rearrange("(c p) n -> p c n", p=P)).then_inc(weights_in, 16)
            sp.dma_start(vbias[:], b_kqv[2 * DM:3 * DM].partition_broadcast(P)).then_inc(weights_in, 16)
            sp.dma_start(pbias[:], b_proj.partition_broadcast(P)).then_inc(weights_in, 16)
            for n in range(2):
                sp.wait_ge(gathered[n], 64)
            sp.wait_ge(zeros_ready, 1)
            sp.dma_start(xrow[NTOK:NTOK + CAP, :].rearrange("(c p) w -> p c w", p=P), zeros[:]).then_inc(spare_out, 16)
            sp.dma_start(out[NTOK:NTOK + CAP, :].rearrange("(c p) w -> p c w", p=P),
                         zeros[:, :, 0:DM]).then_inc(spare_out, 16)

            def load(e, p, t):
                if not (known(e) and e < 2):
                    wait(sp, guT_done, e - 1)
                    wait(sp, dnT_done, e - 1)
                rows = gate_up_proj[bass.ds(e, 1), :, :].rearrange("e (a f) h -> f (e a) h", a=2)
                sp.dma_start(gu[:, p, 0:3:2, :], rows[0:P, :, :]).then_inc(gu_in[p], 16)
                for a in range(2):
                    sp.dma_start(gu[a * F1:(a + 1) * F1, p, 1, :], rows[P:F, a, :]).then_inc(gu_in[p], 16)
                sp.dma_start(dn[:, p, :, :], down_proj[bass.ds(e, 1), :, :].rearrange("e (c p) f -> p (e c) f", p=P)
                             ).then_inc(dn_in[p], 16)

            load(0, 0, 0)
            load(1, 1, 0)

            def step(i, par, has):
                if has(-3):
                    b, p = i - 3, 1 - par
                    wait(sp, row_ready, b + 1)
                    sp.dma_start(xrow[bass.ds(b * S, S), :], xr[:, p, :]).then_inc(row_out[p], 16)
                if has(-1):
                    b, p = i - 1, 1 - par
                    wait(sp, h1_ready, b + 1)
                    sp.dma_start(out[bass.ds(b * S, S), :], h1[:, p, :]).then_inc(h1_out[p], 16)
                if known(i) and i - 3 == NB - 1:
                    for n in range(2):
                        sp.wait_ge(cnt_out[n], 16 * ((NB - n) // 2))
                    sp.dma_start(cum[0:NB - 1, :, :], counts_dram[0:NB - 1, :, :]).then_inc(cum_in, 16)
                    sp.dma_start(cum_p[1:NB, :, :], counts_dram[0:NB - 1, :, :]).then_inc(cum_in, 16)
                    sp.wait_ge(cnt_copied, NB)
                    sp.dma_start(cum[NB - 1:NB, :, :], cnt[:, 1 - par, :]).then_inc(cum_in, 16)
                elif has(-3):
                    b, p = i - 3, 1 - par
                    wait(sp, cnt_copied, b + 1)
                    sp.dma_start(counts_dram[bass.ds(b, 1), :, :].rearrange("b e s -> e (b s)"),
                                 cnt[:, p, :]).then_inc(cnt_out[p], 16)

            steps(sp, step)

            with sp.Fori(1, NE // 2) as t:
                for p in range(2):
                    load(2 * t + p, p, t)
            for n in range(2):
                sp.wait_ge(added[n], 16 * CC * NE // 2)

        @block.gpsimd
        def _(pool):
            nc.gpsimd.memset(ident[:], 0.0).then_inc(pool_step, 1)
            nc.gpsimd.memset(upper_f[:], 1.0).then_inc(pool_step, 1)
            nc.gpsimd.memset(minus_half[:], -0.5)
            nc.gpsimd.iota(rel_i[:], pattern=[[1, S]], base=0, channel_multiplier=-1)
            nc.gpsimd.iota(part_i[:], pattern=[[0, 1]], base=0, channel_multiplier=1)
            nc.gpsimd.iota(slot_i[:], pattern=[[1, CAP]], base=0, channel_multiplier=0)
            nc.gpsimd.iota(seq_i[:], pattern=[[0, 1]], base=0, channel_multiplier=P)
            nc.gpsimd.iota(slotp_i[:], pattern=[[P, CC]], base=0, channel_multiplier=1)
            pool.wait_ge(pool_step, 2)
            nc.gpsimd.affine_select(out=ident[:], in_=ident[:], compare_op=ALU.not_equal, fill=1.0, base=0,
                                    pattern=[[-1, P]], channel_multiplier=1)
            nc.gpsimd.affine_select(out=upper_f[:], in_=upper_f[:], compare_op=ALU.is_ge, fill=0.0, base=0,
                                    pattern=[[1, P]], channel_multiplier=-1).then_inc(pool_const, 1)

            def prepare_gather(b, p, t):
                wait(pool, embT_done, b - 1)
                wait(pool, gathered[p], 64 * t)
                nc.gpsimd.tensor_copy(idx[:, p, :], ids_all[:, bass.ds(b, 1), :].rearrange("p b n -> p (b n)")
                                      ).then_inc(idx_copied, 1)
                nc.gpsimd.memset(emb[:, p, :], 0.0).then_inc(emb_clear, 1)
                wait(pool, emb_clear, b + 1)
                wait(pool, idx_copied, b + 1)

            def gather(p):
                for n in range(4):
                    nc.gpsimd.indirect_dma_start(
                        out=emb[:, p, STARTS[n]:STARTS[n] + WIDTHS[n]], out_offset=None, in_=EMBS[n],
                        in_offset=bass.IndirectOffsetOnAxis(ap=idx[:, p, n:n + 1], axis=0),
                        bounds_check=EMBS[n].shape[0] - 1, oob_is_err=False).then_inc(gathered[p], 16)

            def step(i, par, has, t):
                if has(3):
                    prepare_gather(i + 3, 1 - par, t(3))
                if has(0):
                    b, p = i, par
                    wait(pool, h_copied, b + 1)
                    wait(pool, h1_ready, b - 1)
                    nc.gpsimd.tensor_tensor(hb[:, p, :], h_all[:, bass.ds(b, 1), :].rearrange("p b n -> p (b n)"),
                                            pbias[:], ALU.add).then_inc(hb_ready, 1)
                if has(3):
                    gather(1 - par)
                if has(2):
                    b, p = i + 2, par
                    wait(pool, var1_ready, b + 1)
                    nc.gpsimd.tensor_tensor(rs1[:, p, :], ve1[:, p, :], minus_half[:], ALU.pow).then_inc(rs1_ready, 1)
                if has(1):
                    b, p = i + 1, 1 - par
                    wait(pool, qk_hi_ready, b + 1)
                    nc.gpsimd.tensor_tensor(k_lo[:, p, :, :, :], kT[:, p, :, :, :], k_hi[:, p, :, :, :], ALU.subtract
                                            ).then_inc(k_lo_ready, 1)
                if has(-1):
                    b, p = i - 1, 1 - par
                    wait(pool, var2_ready, b + 1)
                    nc.gpsimd.tensor_tensor(rs2[:, p, :], ve2[:, p, :], minus_half[:], ALU.pow).then_inc(rs2_ready, 1)

            pool.wait_ge(ids_ready, 1)
            for i in range(-AHEAD, FULL_LO):
                if i == 0:
                    pool.wait_ge(weights_in, 64)
                step(i, i % 2, lambda lag, i=i: 0 <= i + lag < NB, lambda lag, i=i: (i + lag) // 2)
            with pool.Fori(FULL_LO // 2, FULL_HI // 2) as t:
                for par in range(2):
                    step(2 * t + par, par, lambda lag: True, lambda lag: t + (par + lag) // 2)
            for i in range(FULL_HI, NB + BEHIND):
                step(i, i % 2, lambda lag, i=i: 0 <= i + lag < NB, lambda lag, i=i: (i + lag) // 2)

            for n in range(2):
                pool.wait_ge(row_out[n], 16 * NB // 2)
                pool.wait_ge(h1_out[n], 16 * NB // 2)

            def fetch(e, p, t):
                wait(pool, rows_ready, e + 1)
                wait(pool, xg_in[p], 16 * CC * t)
                wait(pool, xgT_done, e - 1)
                wait(pool, wcol_ready, e - 1)
                nc.gpsimd.tensor_copy(gidx[:, p, :], rows_all[:, bass.ds(e, 1), :].rearrange("p e c -> p (e c)")
                                      ).then_inc(gidx_copied, 1)
                pool.wait_ge(spare_out, 32)
                wait(pool, gidx_copied, e + 1)
                for c in range(CC):
                    nc.gpsimd.indirect_dma_start(
                        out=xg[:, p, c, :], out_offset=None, in_=xrow,
                        in_offset=bass.IndirectOffsetOnAxis(ap=gidx[:, p, c:c + 1], axis=0),
                        bounds_check=NTOK + CAP - 1, oob_is_err=False).then_inc(xg_in[p], 16)

            def add(e, p, t):
                wait(pool, added[1 - p], 16 * CC * (t + p))
                nc.gpsimd.tensor_copy(sidx[:, p, :], rows_all[:, bass.ds(e, 1), :].rearrange("p e c -> p (e c)")
                                      ).then_inc(sidx_copied, 1)
                pool.wait_ge(spare_out, 32)
                wait(pool, eo_ready, e + 1)
                wait(pool, sidx_copied, e + 1)
                for c in range(CC):
                    nc.gpsimd.indirect_dma_start(
                        out=out, out_offset=bass.IndirectOffsetOnAxis(ap=sidx[:, p, c:c + 1], axis=0),
                        in_=eo[:, p, c, :], in_offset=None, bounds_check=NTOK + CAP - 1, oob_is_err=True,
                        compute_op=ALU.add).then_inc(added[p], 16)

            fetch(0, 0, 0)
            fetch(1, 1, 0)
            for p in range(2):
                fetch(2 + p, p, 1)
                add(p, p, 0)
            with pool.Fori(1, NE // 2 - 1) as t:
                for p in range(2):
                    fetch(2 * t + 2 + p, p, t + 1)
                    add(2 * t + p, p, t)
            for p in range(2):
                add(NE - 2 + p, p, NE // 2 - 1)

        @block.scalar
        def _(act):
            def exps(i, p, c):
                wait(act, min_ready, NC * i + c + 1)
                for j in range(HC):
                    last = nc.scalar.activation(sc[:, p, c, j, :], sc[:, p, c, j, :], ACT.Exp,
                                                bias=mn[:, p, c, j:j + 1], scale=-1.0)
                last.then_inc(prob_ready, 1)

            def probT_copy(i, c):
                wait(act, probT_done, NC * i + c + 1)
                wait(act, pv_done, NC * i + c - 1)
                nc.scalar.copy(pT[:, c % 2, :, :], probT_ps[c % 2][:].rearrange("p (j s) -> p j s", j=HC)
                               ).then_inc(probT_copied, 1)

            def step(i, par, has):
                if has(2):
                    b, p = i + 2, par
                    wait(act, embT_done, b + 1)
                    nc.scalar.copy(embT[:, p, 0:KC * P], embT_ps[:, 0:KC * P])
                    nc.scalar.copy(embT[0:ER, p, KC * P:], embT_ps[0:ER, KC * P:(KC + 1) * P]).then_inc(embT_copied, 1)
                if has(0):
                    exps(i, par, 0)
                if has(-3):
                    b, p = i - 3, 1 - par
                    wait(act, nmax_ready, b + 1)
                    nc.scalar.activation(ex[:, p, :], logits[:, p, :], ACT.Exp, bias=nmax[:, p, :]).then_inc(ex_ready, 1)
                if has(2):
                    b = i + 2
                    wait(act, h_done, b + 1)
                    nc.scalar.copy(h_all[:, bass.ds(b, 1), :].rearrange("p b n -> p (b n)"), h_ps).then_inc(h_copied, 1)
                if has(0):
                    exps(i, par, 1)
                if has(1):
                    b, p = i + 1, 1 - par
                    wait(act, ln1T_done, b + 1)
                    nc.scalar.copy(ln1T[:, p, :], ln1T_ps).then_inc(ln1T_copied, 1)
                if has(0):
                    probT_copy(i, 0)
                if has(0):
                    exps(i, par, 2)
                if has(-1):
                    b, p = i - 1, 1 - par
                    wait(act, yT_done, b + 1)
                    nc.scalar.copy(yT[:, p, :], yT_ps).then_inc(yT_copied, 1)
                if has(0):
                    probT_copy(i, 1)
                    exps(i, par, 3)
                    probT_copy(i, 2)
                if has(-2):
                    b, p = i - 2, par
                    wait(act, ln2T_done, b + 1)
                    nc.scalar.copy(ln2T[:, p, :], ln2T_ps).then_inc(ln2T_copied, 1)
                if has(1):
                    b, p = i + 1, 1 - par
                    wait(act, qk_ready, b + 1)
                    nc.scalar.copy(q_hi[:, p, :, :], qT[:, p, :, :])
                    nc.scalar.copy(k_hi[:, p, :, :, :], kT[:, p, :, :, :]).then_inc(qk_hi_ready, 1)
                if has(0):
                    probT_copy(i, 3)

            act.wait_ge(zeros_ready, 1)
            nc.scalar.copy(cum_p[0:1, :, :], zeros[0:1, 0, 0:S].unsqueeze(1).to_broadcast([1, NE, S])).then_inc(cum_clear, 1)
            steps(act, step)

            def gate_up_weights(e, p):
                wait(act, guT_done, e + 1)
                for c in range(KC):
                    last = nc.scalar.copy(guT_hi[:, p, c, :], guT_ps[c][:, 0:F2])
                last.then_inc(guT_rounded, 1)

            def down_weights(e, p):
                wait(act, dnT_done, e + 1)
                nc.scalar.copy(dnT[:, p, 0, :], dnT_ps[:, 0:DM])
                nc.scalar.copy(dnT[0:F1, p, 1, :], dnT_ps[0:F1, DM:2 * DM]).then_inc(dnT_copied, 1)

            def tokens(e, p):
                wait(act, xgT_done, e + 1)
                nc.scalar.copy(xgT_hi[:, p, :, :], xgT_ps[:].rearrange("p (c s) -> p c s", c=KC)).then_inc(xgT_rounded, 1)

            def silus(e):
                wait(act, gate_done, 3 * e + 1)
                wait(act, hT_ready, e)
                nc.scalar.activation(silu_a[:], gate_ps, ACT.Silu)
                wait(act, gate_done, 3 * e + 2)
                nc.scalar.activation(silu_b[:], mixed_ps[0:F1, :], ACT.Silu).then_inc(silu_ready, 1)

            def weigh(e, p, t):
                wait(act, eo_done, e + 1)
                wait(act, wcol_ready, e + 1)
                wait(act, added[p], 16 * CC * t)
                for c in range(CC):
                    last = nc.scalar.activation(eo[:, p, c, :], eo_ps[:, c * DM:(c + 1) * DM], ACT.Copy,
                                                scale=wcol[:, p, c:c + 1])
                last.then_inc(eo_ready, 1)

            def expert(e, p, t):
                if not known(e) or e + 1 < NE:
                    down_weights(e + 1, 1 - p)
                silus(e)
                if not known(e) or e + 1 < NE:
                    tokens(e + 1, 1 - p)
                if not known(e) or e + 2 < NE:
                    gate_up_weights(e + 2, p)
                weigh(e, p, t)

            gate_up_weights(0, 0)
            down_weights(0, 0)
            gate_up_weights(1, 1)
            tokens(0, 0)
            for e in range(2):
                expert(e, e % 2, e // 2)
            with act.Fori(1, NE // 2 - 2) as t:
                for p in range(2):
                    expert(2 * t + p, p, t)
            for e in range(NE - 4, NE):
                expert(e, e % 2, e // 2)

        @block.vector
        def _(dve):
            v = nc.vector
            chain = [0]

            def link(ins):
                chain[0] += 1
                ins.then_inc(dve_step, 1)
                dve.wait_ge(dve_step, chain[0])

            dve.wait_ge(ids_in, 16)
            v.tensor_copy(ids_f[:], ids_rows[:]).then_inc(ids_float, 1)
            v.memset(zeros[:], 0.0).then_inc(zeros_ready, 1)
            v.memset(ones[:], 1.0)
            v.memset(seen[:, 1, :], 0.0)
            v.memset(vv[:, :, :, D:D + 1], 1.0)
            dve.wait_ge(pool_const, 1)
            v.tensor_copy(upper[:], upper_f[:])
            link(v.tensor_copy(rel[:], rel_i[:]))
            dve.wait_ge(setup_T, 1)
            link(v.tensor_copy(ids_t[:], bank[3][:, 0:NB]))
            for n in range(4):
                v.tensor_scalar(low[:, n, :], ids_t[:], float(FIRST_ID[n]), BIG, ALU.is_lt, ALU.mult)
                last = v.tensor_scalar(shifted[:, n, :], ids_t[:], -float(FIRST_ID[n]), None, ALU.add)
            link(last)
            v.tensor_tensor(ids_all[:].rearrange("p b n -> p n b"), low[:], shifted[:], ALU.add).then_inc(ids_ready, 1)
            v.tensor_scalar(later[:], rel[:], 0.0, NEG, ALU.is_gt, ALU.mult)
            link(v.tensor_scalar(part_b[:], part_i[:], D, None, ALU.bitwise_and))
            link(v.tensor_scalar(even[:], part_b[:], 0.0, None, ALU.is_equal))
            v.tensor_scalar(odd[:], even[:], -1.0, 1.0, ALU.mult, ALU.add)
            dve.wait_ge(small_in, 16 * 7)
            link(v.tensor_scalar(slopes_n[:], slopes_b[:], -1.0, None, ALU.mult))
            dve.wait_ge(setup_T, 2)
            v.tensor_copy(projT[:], bank[0][:].rearrange("p (c n) -> p c n", c=KC))
            v.tensor_copy(projT_r[:], bank[1][0:ER, 0:DM]).then_inc(proj_ready, 1)
            v.tensor_copy(gateT[:], bank[2][:, 0:KC * NE].rearrange("p (c n) -> p c n", c=KC))
            link(v.tensor_copy(bias_t[:], bank[2][:, 128:128 + 3 * KC]))
            v.tensor_scalar(qbias[:], bias_t[:, KC:2 * KC], QSCALE, None, ALU.mult)
            v.tensor_scalar(kbias_even[:], bias_t[:, 0:KC], even[:], None, ALU.mult)
            v.tensor_scalar(kbias_odd[:], bias_t[:, 0:KC], odd[:], None, ALU.mult)
            for c in range(NC):
                for j in range(HC):
                    n = head_of(c, j)
                    v.scalar_tensor_tensor(bias_neg[:, c, j, :], rel[:], slopes_n[:, n:n + 1], later[:], ALU.mult, ALU.add)
            dve.wait_ge(weights_in, 64)
            v.tensor_scalar(wq[:], wkqv[:, :, DM:2 * DM], QSCALE, None, ALU.mult).then_inc(setup_ready, 1)
            dve.wait_ge(setup_ready, 1)

            def scores(i, p, c):
                n = NC * i + c
                wait(dve, score_done, n + 1)
                if c == 0:
                    wait(dve, pv_done, NC * (i - 1))
                v.tensor_tensor(sc[:, p, c, :, :], score_ps[c % 2][:].rearrange("p (j s) -> p j s", j=HC),
                                bias_neg[:, c, :, :], ALU.add).then_inc(score_read, 1)

            def minima(i, p, c):
                wait(dve, score_read, NC * i + c + 1)
                v.tensor_reduce(mn[:, p, c, :], sc[:, p, c, :, :], axis=AX.X, op=ALU.min).then_inc(min_ready, 1)

            def step(i, par, has, t):
                b0, p0 = i, par
                b1, p1 = i + 1, 1 - par
                b2, p2 = i + 2, par
                m1, q1 = i - 1, 1 - par
                m2, q2 = i - 2, par
                m3, q3 = i - 3, 1 - par
                if has(0):
                    wait(dve, v_done, b0 + 1)
                    wait(dve, pv_done, NC * (b0 - 1))
                    v.tensor_tensor(vv[:, p0, :, 0:D], v_ps.rearrange("p (h d) -> p h d", h=H),
                                    vbias[:].rearrange("p (h d) -> p h d", h=H), ALU.add).then_inc(v_ready, 1)
                    scores(b0, p0, 0)
                if has(-3):
                    v.max(top8[:, q3, :], logits[:, q3, :]).then_inc(top8_ready, 1)
                if has(0):
                    minima(b0, p0, 0)
                if has(-3):
                    wait(dve, top8_ready, m3 + 1)
                    v.tensor_scalar(nmax[:, q3, :], top8[:, q3, 0:1], -1.0, None, ALU.mult).then_inc(nmax_ready, 1)
                    v.match_replace(rest[:, q3, :], top8[:, q3, :], logits[:, q3, :], -3e38).then_inc(rest_ready, 1)
                if has(0):
                    scores(b0, p0, 1)
                if has(-3):
                    wait(dve, rest_ready, m3 + 1)
                    wait(dve, cnt_done, m3 - 1)
                    v.tensor_tensor(mask[:, q3, :], logits[:, q3, :], rest[:, q3, :], ALU.not_equal).then_inc(mask_ready, 1)
                if has(0):
                    minima(b0, p0, 1)
                if has(-3):
                    wait(dve, mask_ready, m3 + 1)
                    wait(dve, seen_ready, m3)
                    wait(dve, cnt_done, m3)
                    v.tensor_tensor(seen[:, q3, :], seen[:, 1 - q3, :], mask[:, q3, :], ALU.add).then_inc(seen_ready, 1)
                if has(2):
                    wait(dve, h_copied, b2 + 1)
                    v.bn_stats(st1[:, p2, :], h_all[:, bass.ds(b2, 1), :].rearrange("p b n -> p (b n)")).then_inc(st1_done, 1)
                if has(-1):
                    wait(dve, pv_done, NC * (m1 + 1))
                    v.reciprocal(rden[:, q1, :], y_ps[:, :, D:D + 1].rearrange("p h o -> p (h o)")).then_inc(rden_ready, 1)
                if has(-3):
                    wait(dve, ex_ready, m3 + 1)
                    v.scalar_tensor_tensor(exm[:, q3, :], ex[:, q3, :], 1.0, mask[:, q3, :], ALU.mult, ALU.mult,
                                           accum_out=esum[:, q3, :]).then_inc(exm_ready, 1)
                if has(2):
                    wait(dve, st1_done, b2 + 1)
                if has(-1):
                    wait(dve, rden_ready, m1 + 1)
                    wait(dve, yT_done, m1 - 1)
                    v.tensor_tensor(y[:, q1, :].rearrange("p (h d) -> p h d", h=H), y_ps[:, :, 0:D],
                                    rden[:, q1, :].unsqueeze(2).to_broadcast([P, H, D]), ALU.mult).then_inc(y_ready, 1)
                if has(0):
                    scores(b0, p0, 2)
                if has(2):
                    v.bn_aggr(mv1[:, p2, :], st1[:, p2, :]).then_inc(mv1_done, 1)
                if has(-3):
                    wait(dve, exm_ready, m3 + 1)
                    v.reciprocal(rsum[:, q3, :], esum[:, q3, :]).then_inc(rsum_ready, 1)
                if has(0):
                    minima(b0, p0, 2)
                if has(2):
                    wait(dve, mv1_done, b2 + 1)
                    v.tensor_scalar(ve1[:, p2, :], mv1[:, p2, 1:2], EPS, None, ALU.add).then_inc(var1_ready, 1)
                if has(-3):
                    wait(dve, rsum_ready, m3 + 1)
                    v.tensor_scalar(xr[:, q3, DM:XW], exm[:, q3, :], rsum[:, q3, :], None, ALU.mult).then_inc(row_ready, 1)
                if has(0):
                    scores(b0, p0, 3)
                    minima(b0, p0, 3)
                if has(1):
                    wait(dve, qk_done, b1 + 1)
                    wait(dve, score_done, NC * (b1 - 1))
                    v.tensor_tensor(qT[:, p1, :, :], q_ps, qbias[:].unsqueeze(2).to_broadcast([P, KC, S]), ALU.add)
                    v.scalar_tensor_tensor(kT[:, p1, :, 0, :], k_ps, even[:],
                                           kbias_even[:].unsqueeze(2).to_broadcast([P, KC, S]), ALU.mult, ALU.add)
                    v.scalar_tensor_tensor(kT[:, p1, :, 1, :], k_ps, odd[:],
                                           kbias_odd[:].unsqueeze(2).to_broadcast([P, KC, S]), ALU.mult, ALU.add
                                           ).then_inc(qk_ready, 1)
                if has(-1):
                    wait(dve, proj_done, m1 + 1)
                    wait(dve, hb_ready, m1 + 1)
                    wait(dve, h1_out[q1], 16 * t(-1))
                    v.tensor_tensor(h1[:, q1, :], proj_ps, hb[:, q1, :], ALU.add).then_inc(h1_ready, 1)
                if has(1):
                    wait(dve, qk_hi_ready, b1 + 1)
                    v.tensor_tensor(q_lo[:, p1, :, :], qT[:, p1, :, :], q_hi[:, p1, :, :], ALU.subtract).then_inc(q_lo_ready, 1)
                if has(-1):
                    wait(dve, h1_ready, m1 + 1)
                    v.bn_stats(st2[:, q1, :], h1[:, q1, :]).then_inc(st2_done, 1)
                    wait(dve, st2_done, m1 + 1)
                if has(2):
                    wait(dve, rs1_ready, b2 + 1)
                    wait(dve, ln1T_done, b2 - 1)
                    v.tensor_scalar(ln1[:, p2, :], h_all[:, bass.ds(b2, 1), :].rearrange("p b n -> p (b n)"),
                                    mv1[:, p2, 0:1], rs1[:, p2, :], ALU.subtract, ALU.mult).then_inc(ln1_ready, 1)
                if has(-1):
                    v.bn_aggr(mv2[:, q1, :], st2[:, q1, :]).then_inc(mv2_done, 1)
                    wait(dve, mv2_done, m1 + 1)
                    v.tensor_scalar(ve2[:, q1, :], mv2[:, q1, 1:2], EPS, None, ALU.add).then_inc(var2_ready, 1)
                if has(-2):
                    wait(dve, logit_done, m2 + 1)
                    v.tensor_copy(logits[:, q2, :], logit_ps).then_inc(logit_copied, 1)
                    wait(dve, logit_copied, m2 + 1)
                if has(-3):
                    wait(dve, cnt_done, m3 + 1)
                    wait(dve, cnt_out[q3], 16 * t(-3))
                    v.tensor_scalar(cnt[:, q3, :], cnt_ps, float(CAP), None, ALU.min).then_inc(cnt_copied, 1)
                if has(-1):
                    wait(dve, rs2_ready, m1 + 1)
                    wait(dve, row_out[q1], 16 * t(-1))
                    v.tensor_scalar(xr[:, q1, 0:DM], h1[:, q1, :], mv2[:, q1, 0:1], rs2[:, q1, :],
                                    ALU.subtract, ALU.mult).then_inc(ln2_ready, 1)

            for i in range(-AHEAD, FULL_LO):
                step(i, i % 2, lambda lag, i=i: 0 <= i + lag < NB, lambda lag, i=i: (i + lag) // 2)
            with dve.Fori(FULL_LO // 2, FULL_HI // 2) as t:
                for par in range(2):
                    step(2 * t + par, par, lambda lag: True, lambda lag: t + (par + lag) // 2)
            for i in range(FULL_HI, NB + BEHIND):
                step(i, i % 2, lambda lag, i=i: 0 <= i + lag < NB, lambda lag, i=i: (i + lag) // 2)

            def weights(e, p):
                wait(dve, guT_rounded, e + 1)
                for c in range(KC):
                    last = v.tensor_tensor(guT_lo[:, p, c, :], guT_ps[c][:, 0:F2], guT_hi[:, p, c, :], ALU.subtract)
                last.then_inc(guT_copied, 1)

            v.tensor_copy(slot_row[:], slot_i[:])
            v.memset(seq_col[:, 1:2], 1.0)
            v.tensor_copy(seq_col[:, 0:1], seq_i[:])
            v.tensor_copy(slotp[:], slotp_i[:])
            v.tensor_scalar(spare[:], slotp_i[:], float(NTOK - P), None, ALU.add).then_inc(slots_ready, 1)
            dve.wait_ge(slots_ready, 1)
            weights(0, 0)
            dve.wait_ge(cum_in, 48)

            def spread(e, p):
                wait(dve, onehot_ready, e - 1)
                v.tensor_scalar(before[:, p, :], slot_row[:], cum_p[:, bass.ds(e, 1), S - 1:S].rearrange("b e s -> b (e s)"),
                                None, ALU.is_lt).then_inc(before_ready, 1)
                wait(dve, before_ready, e + 1)
                wait(dve, rows_done, e - 1)
                v.scalar_tensor_tensor(onehot[:, p, :], slot_row[:],
                                       cum[:, bass.ds(e, 1), S - 1:S].rearrange("b e s -> b (e s)"),
                                       before[:, p, :], ALU.is_lt, ALU.subtract).then_inc(onehot_ready, 1)

            def number(e, p):
                wait(dve, rows_done, e + 1)
                for c in range(CC):
                    v.tensor_scalar(le[:, p, c, :], cumrow_ps[:, c, :], slotp[:, c:c + 1], None, ALU.is_le, ALU.add,
                                    accum_out=nle[:, p, c:c + 1])
                v.tensor_tensor(t_a[:, p, :], base_ps[:, :, 1], spare[:], ALU.mult).then_inc(row_a, 1)
                wait(dve, row_a, e + 1)
                v.tensor_tensor(t_b[:, p, :], spare[:], t_a[:, p, :], ALU.subtract).then_inc(row_b, 1)
                v.tensor_tensor(t_c[:, p, :], base_ps[:, :, 0], nle[:, p, :], ALU.add).then_inc(row_c, 1)
                wait(dve, row_b, e + 1)
                wait(dve, row_c, e + 1)
                v.tensor_tensor(rows_all[:, bass.ds(e, 1), :].rearrange("p e c -> p (e c)"), t_b[:, p, :], t_c[:, p, :],
                                ALU.add).then_inc(rows_ready, 1)

            def take_weights(e, p, t):
                wait(dve, xg_in[p], 16 * CC * (t + 1))
                wait(dve, eo_ready, e - 1)
                v.tensor_copy(wcol[:, p, :], xg[:, p, :, bass.ds(e + DM, 1)].rearrange("p c o -> p (c o)")
                              ).then_inc(wcol_ready, 1)

            def gates(e):
                wait(dve, silu_ready, e + 1)
                wait(dve, gate_done, 3 * e + 3)
                wait(dve, eo_done, e)
                v.tensor_tensor(hT_a[:], silu_a[:], up_ps, ALU.mult)
                v.tensor_tensor(hT_b[:], silu_b[:], mixed_ps[F1:P, :], ALU.mult).then_inc(hT_ready, 1)

            def tokens_rest(e, p):
                wait(dve, xgT_rounded, e + 1)
                v.tensor_tensor(xgT_lo[:, p, :, :], xgT_ps[:].rearrange("p (c s) -> p c s", c=KC), xgT_hi[:, p, :, :],
                                ALU.subtract).then_inc(xgT_copied, 1)

            spread(0, 0)
            number(0, 0)
            spread(1, 1)
            number(1, 1)
            weights(1, 1)
            spread(2, 0)
            number(2, 0)
            spread(3, 1)
            take_weights(0, 0, 0)
            tokens_rest(0, 0)

            def expert(e, p, t):
                gates(e)
                if not known(e) or e + 1 < NE:
                    take_weights(e + 1, 1 - p, t + p)
                    tokens_rest(e + 1, 1 - p)
                if not known(e) or e + 3 < NE:
                    number(e + 3, 1 - p)
                if not known(e) or e + 2 < NE:
                    weights(e + 2, p)
                if not known(e) or e + 4 < NE:
                    spread(e + 4, p)

            for e in range(2):
                expert(e, e % 2, e // 2)
            with dve.Fori(1, NE // 2 - 2) as t:
                for p in range(2):
                    expert(2 * t + p, p, t)
            for e in range(NE - 4, NE):
                expert(e, e % 2, e // 2)

        @block.tensor
        def _(pe):
            mm, tr = nc.tensor.matmul, nc.tensor.transpose

            def keep_busy(n):
                for _ in range(n):
                    mm(bank[7][:, 3 * P:4 * P], ident[:], ident[:], start=True, stop=True)

            pe.wait_ge(pool_const, 1)
            pe.wait_ge(ids_float, 1)
            tr(bank[3][:, 0:NB], ids_f[:], ident[0:NB, 0:NB]).then_inc(setup_T, 1)
            pe.wait_ge(small_in, 16 * 7)
            for c in range(KC):
                for r in range(KC):
                    tr(bank[0][:, c * DM + r * P:c * DM + (r + 1) * P], proj_rows[:, r, c * P:(c + 1) * P], ident[:])
            for r in range(KC):
                tr(bank[1][0:ER, r * P:(r + 1) * P], proj_rows[:, r, KC * P:EW], ident[:])
                tr(bank[2][:, r * NE:(r + 1) * NE], gate_rows[:, r * P:(r + 1) * P], ident[0:NE, 0:NE])
            tr(bank[2][:, 128:128 + 3 * KC], bias_rows[:], ident[0:3 * KC, 0:3 * KC]).then_inc(setup_T, 1)
            keep_busy(20)
            pe.wait_ge(proj_ready, 1)

            def transposed(dst, src, done):
                for c in range(KC):
                    last = tr(dst[:, c * P:(c + 1) * P], src[:, c * P:(c + 1) * P], ident[:])
                last.then_inc(done, 1)

            def score(i, p, c):
                n = NC * i + c
                if c == 0:
                    wait(pe, q_lo_ready, i + 1)
                    wait(pe, k_lo_ready, i + 1)
                wait(pe, score_read, n - 1)
                if c == 1:
                    wait(pe, v_ready, i + 1)
                rows = slice(2 * D * c, 2 * D * (c + 1))
                parts = ((q_hi, k_hi), (q_lo, k_hi), (q_hi, k_lo))
                for r in range(KC):
                    for n, (q, k) in enumerate(parts):
                        last = mm(score_ps[c % 2][:, r * 2 * S:(r + 1) * 2 * S], q[rows, p, r, :],
                                  k[rows, p, r, :, :].rearrange("p a s -> p (a s)"), start=(n == 0), stop=(n == len(parts) - 1))
                last.then_inc(score_done, 1)

            def probT(i, p, c):
                n = NC * i + c
                wait(pe, prob_ready, n + 1)
                wait(pe, probT_copied, n - 1)
                for j in range(HC):
                    last = tr(probT_ps[c % 2][:, j * S:(j + 1) * S], sc[:, p, c, j, :], ident[:])
                last.then_inc(probT_done, 1)

            def pv(i, p, c):
                if c == 0:
                    wait(pe, v_ready, i + 1)
                    wait(pe, y_ready, i)
                wait(pe, probT_copied, NC * i + c + 1)
                for j in range(HC):
                    n = head_of(c, j)
                    last = mm(y_ps[:, n, :], pT[:, c % 2, j, :], vv[:, p, n, :], start=True, stop=True)
                last.then_inc(pv_done, 1)

            def qk(i, par, n, w):
                b, p = i + 1, 1 - par
                if n == 0:
                    if known(i) and i < 0:
                        keep_busy(4)
                    wait(pe, ln1T_copied, b + 1)
                    wait(pe, score_read, NC * b - 1)
                for r in range(KC):
                    o = (n * KC + r) * S
                    for c in range(KC):
                        last = mm(bank[0][:, o:o + S], w[:, c, r * P:(r + 1) * P],
                                  ln1T[:, p, c * P:(c + 1) * P], start=(c == 0), stop=(c == KC - 1))
                if n == 1:
                    last.then_inc(qk_done, 1)

            def step(i, par, has, t):
                if has(0):
                    wait(pe, ln1T_copied, i + 1)
                    wait(pe, score_read, NC * i)
                    for c in range(KC):
                        last = mm(v_ps, ln1T[:, par, c * P:(c + 1) * P], wkqv[:, c, 2 * DM:3 * DM],
                                  start=(c == 0), stop=(c == KC - 1))
                    last.then_inc(v_done, 1)
                    if known(i) and i < 2:
                        keep_busy(5 if i else 12)
                    score(i, par, 0)
                if has(2):
                    b, p = i + 2, par
                    wait(pe, gathered[p], 64 * (t(2) + 1))
                    wait(pe, h_copied, b)
                    wait(pe, ln2T_copied, b - 4)
                    for c in range(KC):
                        tr(embT_ps[:, c * P:(c + 1) * P], emb[:, p, c * P:(c + 1) * P], ident[:])
                    tr(embT_ps[0:ER, KC * P:(KC + 1) * P], emb[:, p, KC * P:EW], ident[:]).then_inc(embT_done, 1)
                if has(-1):
                    pv(i - 1, 1 - par, 2)
                if has(0):
                    score(i, par, 1)
                if has(2):
                    b, p = i + 2, par
                    if known(i) and i < 0:
                        keep_busy(4)
                    wait(pe, embT_copied, b + 1)
                    for c in range(KC):
                        mm(h_ps, embT[:, p, c * P:(c + 1) * P], projT[:, c, :], start=(c == 0), stop=False)
                    mm(h_ps, embT[0:ER, p, KC * P:(KC + 1) * P], projT_r[:], start=False, stop=True).then_inc(h_done, 1)
                if has(-1):
                    pv(i - 1, 1 - par, 3)
                if has(0):
                    score(i, par, 2)
                if has(1):
                    b, p = i + 1, 1 - par
                    wait(pe, ln1_ready, b + 1)
                    wait(pe, yT_copied, b - 2)
                    transposed(ln1T_ps, ln1[:, p, :], ln1T_done)
                if has(0):
                    probT(i, par, 0)
                if has(0):
                    score(i, par, 3)
                if has(1):
                    qk(i, par, 0, wq)
                if has(-1):
                    b, p = i - 1, 1 - par
                    wait(pe, y_ready, b + 1)
                    wait(pe, ln1T_copied, min(b + 3, NB) if known(b) else b + 3)
                    transposed(yT_ps, y[:, p, :], yT_done)
                if has(0):
                    probT(i, par, 1)
                if has(1):
                    qk(i, par, 1, wkqv)
                if has(0):
                    pv(i, par, 0)
                    probT(i, par, 2)
                if has(-2):
                    b, p = i - 2, par
                    wait(pe, ln2_ready, b + 1)
                    wait(pe, h_copied, NB if known(b) and b + 5 > NB else b + 5)
                    transposed(ln2T_ps, xr[:, p, 0:DM], ln2T_done)
                if has(-1):
                    b, p = i - 1, 1 - par
                    wait(pe, yT_copied, b + 1)
                    wait(pe, h1_ready, b)
                    wait(pe, logit_copied, b - 1)
                    wait(pe, cnt_copied, b - 2)
                    for c in range(KC):
                        last = mm(proj_ps, yT[:, p, c * P:(c + 1) * P], wproj[:, c, :], start=(c == 0), stop=(c == KC - 1))
                    last.then_inc(proj_done, 1)
                if has(0):
                    pv(i, par, 1)
                if has(0):
                    probT(i, par, 3)
                if has(-3):
                    b, p = i - 3, 1 - par
                    wait(pe, seen_ready, b + 1)
                    wait(pe, cnt_copied, b)
                    wait(pe, logit_copied, b + 1)
                    wait(pe, h1_ready, min(b + 3, NB) if known(b) else b + 3)
                    mm(cnt_ps, mask[:, p, :], upper[:], start=True, stop=False)
                    mm(cnt_ps, seen[:, 1 - p, :], ones[:], start=False, stop=True).then_inc(cnt_done, 1)
                if has(-2):
                    b, p = i - 2, par
                    wait(pe, ln2T_copied, b + 1)
                    wait(pe, logit_copied, b)
                    wait(pe, cnt_copied, b - 1)
                    wait(pe, h1_ready, min(b + 2, NB) if known(b) else b + 2)
                    for c in range(KC):
                        last = mm(logit_ps, ln2T[:, p, c * P:(c + 1) * P], gateT[:, c, :], start=(c == 0), stop=(c == KC - 1))
                    last.then_inc(logit_done, 1)

            for i in range(-AHEAD, FULL_LO):
                if i == -1:
                    pe.wait_ge(setup_ready, 1)
                step(i, i % 2, lambda lag, i=i: 0 <= i + lag < NB, lambda lag, i=i: (i + lag) // 2)
            with pe.Fori(FULL_LO // 2, FULL_HI // 2) as t:
                for par in range(2):
                    step(2 * t + par, par, lambda lag: True, lambda lag: t + (par + lag) // 2)
            for i in range(FULL_HI, NB + BEHIND):
                step(i, i % 2, lambda lag, i=i: 0 <= i + lag < NB, lambda lag, i=i: (i + lag) // 2)

            pe.wait_ge(cnt_copied, NB)

            def rows(e, p):
                wait(pe, onehot_ready, e + 1)
                wait(pe, rows_ready, e)
                wait(pe, hT_ready, e - 2)
                for c in range(CC):
                    mm(cumrow_ps[:, c, :], onehot[:, p, c * P:(c + 1) * P],
                       cum[:, bass.ds(e, 1), :].rearrange("b e s -> b (e s)"), start=True, stop=True)
                for c in range(CC):
                    last = mm(base_ps[:, c, :], onehot[:, p, c * P:(c + 1) * P], seq_col[:], start=True, stop=True)
                last.then_inc(rows_done, 1)

            def gate_upT(e, p, t):
                wait(pe, gu_in[p], 48 * (t + 1))
                wait(pe, guT_copied, e)
                for c in range(KC):
                    for m in range(F2 // P):
                        last = tr(guT_ps[c][:, m * P:(m + 1) * P], gu[:, p, m, c * P:(c + 1) * P], ident[:])
                last.then_inc(guT_done, 1)

            def downT(e, p, t):
                wait(pe, dn_in[p], 16 * (t + 1))
                wait(pe, dnT_copied, e)
                for c in range(KC):
                    tr(dnT_ps[:, c * P:(c + 1) * P], dn[:, p, c, 0:P], ident[:])
                    last = tr(dnT_ps[0:F1, DM + c * P:DM + (c + 1) * P], dn[:, p, c, P:F], ident[:])
                last.then_inc(dnT_done, 1)

            def tokensT(e, p, t):
                wait(pe, xg_in[p], 16 * CC * (t + 1))
                wait(pe, xgT_copied, e)
                for k in range(KC):
                    for c in range(CC):
                        last = tr(xgT_ps[:, k * CAP + c * P:k * CAP + (c + 1) * P], xg[:, p, c, k * P:(k + 1) * P], ident[:])
                last.then_inc(xgT_done, 1)

            def gate_up(e, p):
                wait(pe, guT_copied, e + 1)
                wait(pe, xgT_copied, e + 1)
                wait(pe, hT_ready, e)
                parts = [(w, x, k) for k in range(KC)
                         for w, x in ((guT_hi, xgT_hi), (guT_lo, xgT_hi), (guT_hi, xgT_lo))]
                for m, dst in enumerate((gate_ps, mixed_ps, up_ps)):
                    if m == 1:
                        wait(pe, rows_ready, min(e + 3, NE) if known(e) else e + 3)
                    for n, (w, x, k) in enumerate(parts):
                        last = mm(dst, w[:, p, k, m * P:(m + 1) * P], x[:, p, k, :], start=(n == 0), stop=(n == len(parts) - 1))
                    last.then_inc(gate_done, 1)

            def down(e, p):
                wait(pe, dnT_copied, e + 1)
                wait(pe, hT_ready, e + 1)
                wait(pe, eo_ready, e)
                for c in range(CC):
                    cs = slice(c * P, (c + 1) * P)
                    o = eo_ps[:, c * DM:(c + 1) * DM]
                    mm(o, hT_a[:, cs], dnT[:, p, 0, :], start=True, stop=False)
                    last = mm(o, hT_b[:, cs], dnT[0:F1, p, 1, :], start=False, stop=True)
                last.then_inc(eo_done, 1)

            gate_upT(0, 0, 0)
            downT(0, 0, 0)
            pe.wait_ge(cum_in, 48)
            rows(0, 0)
            rows(1, 1)
            gate_upT(1, 1, 0)
            rows(2, 0)
            tokensT(0, 0, 0)

            def expert(e, p, t):
                if not known(e) or e + 1 < NE:
                    downT(e + 1, 1 - p, t + p)
                gate_up(e, p)
                if not known(e) or e + 1 < NE:
                    tokensT(e + 1, 1 - p, t + p)
                if not known(e) or e + 2 < NE:
                    gate_upT(e + 2, p, t + 1)
                if not known(e) or e + 3 < NE:
                    rows(e + 3, 1 - p)
                down(e, p)

            for e in range(2):
                expert(e, e % 2, e // 2)
            with pe.Fori(1, NE // 2 - 2) as t:
                for p in range(2):
                    expert(2 * t + p, p, t)
            for e in range(NE - 4, NE):
                expert(e, e % 2, e // 2)


_INS = ['x', 'L0_tok_emb0', 'L0_tok_emb1', 'L0_tok_emb2', 'L0_tok_emb3', 'L0_tok_proj0', 'L0_tok_proj1', 'L0_tok_proj2',
        'L0_tok_proj3', 'L0_attn_W_kqv', 'L0_attn_b_kqv', 'L0_attn_W_proj', 'L0_attn_b_proj', 'L0_attn_slopes',
        'L0_ffn_gate_weight', 'L0_ffn_gate_up_proj', 'L0_ffn_down_proj']
_SPARE = 256


def kernel(**inputs):
    import numpy as _np
    import concourse.bacc as _bacc
    from concourse import mybir as _mybir
    from concourse.bass_utils import run_bass_kernel_spmd as _run

    nc = _bacc.Bacc("TRN2", target_bir_lowering=False, num_devices=1)
    arrays, args = {}, []
    for name in _INS:
        a = _np.ascontiguousarray(inputs[name])
        arrays[f"in_{name}_dram"] = a
        args.append(nc.dram_tensor(f"in_{name}_dram", a.shape, _mybir.dt.from_np(a.dtype), kind="ExternalInput").ap())
    nb, s = inputs['x'].shape
    dm = inputs['L0_tok_emb0'].shape[1]
    args.append(nc.dram_tensor("out_0_dram", (nb * s + _SPARE, dm), _mybir.dt.float32, kind="ExternalOutput").ap())
    bass_lm_tower_kernel(nc, *args)
    r = _run(nc, [arrays], core_ids=[0])
    return r.results[0]["out_0_dram"][0:nb * s].reshape(nb, s, dm)
```
